# Optimizing a Trainium2 kernel written in Bass

```python
import numpy as np
import jax
import jax.numpy as jnp

def _softmax(x, axis=-1):
    return jax.nn.softmax(x, axis=axis)

def _gelu(x):
    return jax.nn.gelu(x, approximate=True)

def _silu(x):
    return jax.nn.silu(x)

def _sigmoid(x):
    return jax.nn.sigmoid(x)

def _layernorm(x, axis=-1, eps=1e-05):
    m = jnp.mean(x, axis=axis, keepdims=True)
    v = jnp.var(x, axis=axis, keepdims=True)
    return (x - m) / jnp.sqrt(v + eps)

def _scatter_add(tgt, idx, src, axis=0):
    return tgt.at[idx].add(src)

def _segment_sum(src, seg, n):
    return jax.ops.segment_sum(src, seg, n)
kernel_name = 'mk_gnn_preln_d2_gnn_r8_55517b'

def setup_inputs(seed: int=0):
    np.random.seed(seed)
    _w = jnp.asarray

    def _rec_inputs():
        import jax
        import jax.numpy as jnp
        _gk = jax.random.key(seed)
        x = -8.776e-05 + 1 * jax.random.normal(jax.random.fold_in(_gk, 1), (6250, 256), jnp.float32)
        _s = jax.random.randint(jax.random.fold_in(_gk, 2), (50000,), 0, 6250, jnp.int32)
        _d = jax.random.randint(jax.random.fold_in(_gk, 3), (50000,), 0, 6250, jnp.int32)
        _loop = jnp.arange(6250, dtype=jnp.int32)
        src = jnp.concatenate([_s, _d, _loop])
        dst = jnp.concatenate([_d, _s, _loop])
        _o = jnp.argsort(dst, stable=True)
        src = src[_o]
        dst = dst[_o]
        edge_attr_2 = jax.random.uniform(jax.random.fold_in(_gk, 11), (106250, 2), jnp.float32, 0.0, 1)
        edge_attr_256 = 2.93046e-05 + 1.00006 * jax.random.normal(jax.random.fold_in(_gk, 12), (106250, 256), jnp.float32)
        return (x, src, dst, edge_attr_2, edge_attr_256)
    x, src, dst, edge_attr_2, edge_attr_256 = _rec_inputs()

    def _L0_gnn_setup():
        import jax, jax.numpy as jnp
        import numpy as np
        N, E, D = (2500, 40000, 256)
        H, C = (8, 32)
        key = jax.random.key(seed)
        ks = jax.random.split(key, 12)
        s = 1.0 / np.sqrt(D)
        return {'x': jax.random.normal(ks[0], (N, D), jnp.float32), 'edge_index': jax.random.randint(ks[1], (2, E), 0, N, jnp.int64), 'edge_attr': jax.random.normal(ks[2], (E, D), jnp.float32), 'Wq': jax.random.normal(ks[3], (D, H * C), jnp.float32) * s, 'bq': jnp.zeros((H * C,), jnp.float32), 'Wk': jax.random.normal(ks[4], (D, H * C), jnp.float32) * s, 'bk': jnp.zeros((H * C,), jnp.float32), 'Wv': jax.random.normal(ks[5], (D, H * C), jnp.float32) * s, 'bv': jnp.zeros((H * C,), jnp.float32), 'We': jax.random.normal(ks[6], (D, H * C), jnp.float32) * s, 'Ws': jax.random.normal(ks[7], (D, H * C), jnp.float32) * s, 'bs': jnp.zeros((H * C,), jnp.float32)}
    _L0_gnn_all = _L0_gnn_setup()
    _L0_gnn_in = {k: v for k, v in _L0_gnn_all.items() if k in ('Wq', 'bq', 'Wk', 'bk', 'Wv', 'bv', 'We', 'Ws', 'bs')}
    del _L0_gnn_all

    def _L1_gnn_setup():
        import jax, jax.numpy as jnp
        import numpy as np
        N_NODES = 12500
        N_EDGES = 200000
        IN_FEATS = 256
        OUT_FEATS = 64
        NUM_HEADS = 4
        key = jax.random.key(seed)
        k_h, k_adj, k_dir, k_wf, k_wr, k_af = jax.random.split(key, 6)
        h = jax.random.normal(k_h, (N_NODES, IN_FEATS), dtype=jnp.float32)
        adj = jax.random.randint(k_adj, (2, N_EDGES), 0, N_NODES, dtype=jnp.int64)
        bit = jax.random.randint(k_dir, (N_EDGES,), 0, 2).astype(jnp.float32)
        direction = jnp.stack([bit, 1.0 - bit], axis=1)
        s_w = float(np.sqrt(6.0 / (IN_FEATS + OUT_FEATS)))
        s_a = float(np.sqrt(6.0 / (NUM_HEADS + OUT_FEATS)))
        W_forward = jax.random.uniform(k_wf, (OUT_FEATS, IN_FEATS), jnp.float32, -s_w, s_w)
        W_reverse = jax.random.uniform(k_wr, (OUT_FEATS, IN_FEATS), jnp.float32, -s_w, s_w)
        attn_forward = jax.random.uniform(k_af, (1, NUM_HEADS, OUT_FEATS), jnp.float32, -s_a, s_a)
        return {'h': h, 'adj': adj, 'direction': direction, 'W_forward': W_forward, 'W_reverse': W_reverse, 'attn_forward': attn_forward}
    _L1_gnn_all = _L1_gnn_setup()
    _L1_gnn_in = {k: v for k, v in _L1_gnn_all.items() if k in ('W_forward', 'W_reverse', 'attn_forward')}
    del _L1_gnn_all
    return {'x': x, 'src': src, 'dst': dst, 'edge_attr_2': edge_attr_2, 'edge_attr_256': edge_attr_256, 'L0_gnn_Wq': _L0_gnn_in['Wq'], 'L0_gnn_bq': _L0_gnn_in['bq'], 'L0_gnn_Wk': _L0_gnn_in['Wk'], 'L0_gnn_bk': _L0_gnn_in['bk'], 'L0_gnn_Wv': _L0_gnn_in['Wv'], 'L0_gnn_bv': _L0_gnn_in['bv'], 'L0_gnn_We': _L0_gnn_in['We'], 'L0_gnn_Ws': _L0_gnn_in['Ws'], 'L0_gnn_bs': _L0_gnn_in['bs'], 'L1_gnn_W_forward': _L1_gnn_in['W_forward'], 'L1_gnn_W_reverse': _L1_gnn_in['W_reverse'], 'L1_gnn_attn_forward': _L1_gnn_in['attn_forward']}

def reference(x, src, dst, edge_attr_2, edge_attr_256, L0_gnn_Wq, L0_gnn_bq, L0_gnn_Wk, L0_gnn_bk, L0_gnn_Wv, L0_gnn_bv, L0_gnn_We, L0_gnn_Ws, L0_gnn_bs, L1_gnn_W_forward, L1_gnn_W_reverse, L1_gnn_attn_forward):
    import jax
    import jax.numpy as jnp

    def _L0_gnn_ref(x, edge_index, edge_attr, Wq, bq, Wk, bk, Wv, bv, We, Ws, bs):
        import jax, jax.numpy as jnp
        import numpy as np
        N, E, D = (2500, 40000, 256)
        H, C = (8, 32)
        n = x.shape[0]
        src, dst = (edge_index[0], edge_index[1])
        q = (x @ Wq + bq).reshape(n, H, C)
        k = (x @ Wk + bk).reshape(n, H, C)
        v = (x @ Wv + bv).reshape(n, H, C)
        e = (edge_attr @ We).reshape(-1, H, C)
        kj = k[src] + e
        alpha = jnp.einsum('ehc,ehc->eh', q[dst], kj) / jnp.sqrt(jnp.float32(C))
        amax = jax.ops.segment_max(alpha, dst, num_segments=n)
        ea = jnp.exp(alpha - amax[dst])
        denom = jax.ops.segment_sum(ea, dst, num_segments=n)
        alpha = ea / (denom[dst] + 1e-16)
        msg = (v[src] + e) * alpha[:, :, None]
        out = jax.ops.segment_sum(msg, dst, num_segments=n)
        out = out.reshape(n, H * C) + (x @ Ws + bs)
        return out

    def _L1_gnn_ref(h, adj, direction, W_forward, W_reverse, attn_forward):
        import jax, jax.numpy as jnp
        import numpy as np
        N_NODES = 12500
        N_EDGES = 200000
        IN_FEATS = 256
        OUT_FEATS = 64
        NUM_HEADS = 4
        N = h.shape[0]
        H = attn_forward.shape[1]
        h_fwd = h @ W_forward.T
        h_rev = h @ W_reverse.T
        src, dst = (adj[0], adj[1])
        messages = h_fwd[src] * direction[:, 0:1] + h_rev[src] * direction[:, 1:2]
        scores = jnp.einsum('ef,hf->eh', messages, attn_forward[0])
        scores = jax.nn.leaky_relu(scores, negative_slope=0.2)
        exp_scores = jnp.exp(scores - scores.max(axis=0, keepdims=True))
        sum_exp = jax.ops.segment_sum(exp_scores, dst, num_segments=N)
        norm = exp_scores / (sum_exp[dst] + 1e-10)
        outs = [jax.ops.segment_sum(messages * norm[:, hd:hd + 1], dst, num_segments=N) for hd in range(H)]
        out = jnp.stack(outs, axis=1)
        return out.reshape(N, -1)
    edge_index = jnp.stack([src, dst])
    h = jnp.maximum(_layernorm(x, axis=-1), 0.0)
    x = x + _L0_gnn_ref(h, edge_index, edge_attr_256, L0_gnn_Wq, L0_gnn_bq, L0_gnn_Wk, L0_gnn_bk, L0_gnn_Wv, L0_gnn_bv, L0_gnn_We, L0_gnn_Ws, L0_gnn_bs)
    h = jnp.maximum(_layernorm(x, axis=-1), 0.0)
    x = x + _L1_gnn_ref(h, edge_index, edge_attr_2, L1_gnn_W_forward, L1_gnn_W_reverse, L1_gnn_attn_forward)
    return x

_drawn_inputs = setup_inputs


def setup_inputs(seed=0):
    import zlib

    import numpy as np

    out = dict(_drawn_inputs(seed))
    spreads = {'L0_gnn_bq': (0.0, 0.1),
     'L0_gnn_bk': (0.0, 0.1),
     'L0_gnn_bv': (0.0, 0.1),
     'L0_gnn_bs': (0.0, 0.1)}
    factors = {}
    for name, (base, spread) in spreads.items():
        noise = np.random.default_rng([zlib.crc32(name.encode()), seed]).standard_normal(out[name].shape)
        drawn = base * np.exp(spread * noise) if base else spread * noise
        out[name] = jnp.asarray(drawn.astype(out[name].dtype))
    for name, factor in factors.items():
        out[name] = (out[name] * factor).astype(out[name].dtype)
    return out
```

```python
from contextlib import ExitStack

import concourse.bass as bass
from concourse import mybir

P = 128
N, E, D = 6250, 106250, 256
NT = (N + P - 1) // P
NPAD = NT * P
LAST_NODES = N - (NT - 1) * P
G = 8
ROWS = G * P
STEP = ROWS - 1
NG = (E - 1 + STEP - 1) // STEP
LAST_ROWS = E - (NG - 1) * STEP
PAD_DST = 8191.0
FAR = -1e38
TABW = 264
MSGW = TABW + 1
ALL_ROUNDS = ROWS // P
assert NG <= P and LAST_ROWS < ROWS and NG % 2 == 0

RANK, DIDX, END, DIR0, DIR1 = range(5)
NF = 5

ALU = mybir.AluOpType
ACT = mybir.ActivationFunctionType
AX = mybir.AxisListType
F32 = mybir.dt.float32
I32 = mybir.dt.int32


def at_least(eng, sem, value):
    if isinstance(value, int) and value <= 0:
        return
    eng.wait_ge(sem, value)


def hold(eng, sem, value, passed):
    at_least(eng, sem, value)
    if not isinstance(value, int):
        eng.sem_inc(passed, 1)


def sweep(eng, body, first, last, stop):
    for i in range(first):
        body(i, i % 2)
    with eng.Fori(first // 2, last // 2) as turn_:
        body(turn_ * 2, 0)
        body(turn_ * 2 + 1, 1)
    for i in range(last, stop):
        body(i, i % 2)


def uses(g, parity, per_use):
    return (g - parity) * (per_use // 2) + per_use


class Scope:

    def __init__(self, nc, ctx):
        self.nc, self.ctx = nc, ctx

    def sb(self, name, shape, dt=F32):
        return self.ctx.enter_context(self.nc.sbuf_tensor(name, shape, dt))

    def ps(self, name, shape):
        return self.ctx.enter_context(self.nc.psum_tensor(name, shape, F32))

    def sem(self, name):
        return self.ctx.enter_context(self.nc.semaphore(name))


def prepare_edges(nc, keep, src, dst, edge_attr_2, pen_d, tab0, tab1):
    with ExitStack() as ctx:
        m = Scope(nc, ctx)
        srci, dsti = m.sb("srci", [P, ROWS], I32), m.sb("dsti", [P, ROWS], I32)
        srcf, dstf, dstc = m.sb("srcf", [P, ROWS]), m.sb("dstf", [P, ROWS]), m.sb("dstc", [P, ROWS])
        dirs = m.sb("dirs", [P, ROWS, 2])
        cut = m.sb("cut", [P, ROWS + 1])
        pen = m.sb("pen", [P, ROWS + 1])
        rank, didx = m.sb("rank", [P, ROWS]), m.sb("didx", [P, ROWS])
        empty = m.sb("empty", [P, 2, TABW])
        topf, topi = m.sb("topf", [1, 2]), keep["top"]
        pt = [m.ps(f"pt{b}", [P, 512]) for b in range(2)]
        s_clear, s_load, s_cols, s_pen = m.sem("s_clear"), m.sem("s_load"), m.sem("s_cols"), m.sem("s_pen")
        s_cut, s_id, s_tr, s_ev = m.sem("s_cut"), m.sem("s_id"), m.sem("s_tr"), m.sem("s_ev")
        s_top, s_empty, s_tab = m.sem("s_top"), m.sem("s_empty"), m.sem("s_tab")
        ident, metaf, metai = keep["ident"], keep["metaf"], keep["metai"]

        floats = {RANK: rank[:, :], DIDX: didx[:, :], END: cut[:, 1:ROWS + 1],
                  DIR0: dirs[:, :, 0], DIR1: dirs[:, :, 1]}
        jobs = []
        for half in range(2):
            for k, a in floats.items():
                out = metaf[:, :, k * G + 4 * half:k * G + 4 * half + 4].rearrange("p g t -> p t g")
                jobs.append((a, half, out))
            for k, a in ((0, srcf[:, :]), (1, dstc[:, :])):
                out = metai[:, :, 4 * half:4 * half + 4, k].rearrange("p g t -> p t g")
                jobs.append((a, half, out))
        block = ctx.enter_context(nc.Block())

        @block.sync
        def _(sp):
            sp.wait_ge(s_clear, 3)
            for flat, tile, w in ((src, srci[:, :], 1), (dst, dsti[:, :], 1),
                                  (edge_attr_2.rearrange("e c -> (e c)"), dirs[:, :, :].rearrange("p r c -> p (r c)"), 2)):
                rows = bass.AP(tensor=flat.tensor, offset=0, ap=[[STEP * w, NG - 1], [1, ROWS * w]])
                sp.dma_start(tile[0:NG - 1, :], rows).then_inc(s_load, 16)
                tail = flat[(NG - 1) * STEP * w:E * w].rearrange("(a b) -> a b", a=1)
                sp.dma_start(tile[NG - 1:NG, 0:LAST_ROWS * w], tail).then_inc(s_load, 16)
            sp.wait_ge(s_empty, 2)
            for k, tab in enumerate((tab0, tab1)):
                sp.dma_start(tab.rearrange("(p t) d -> p t d", p=P),
                             empty[:, k, :].unsqueeze(1).to_broadcast([P, NT, TABW])).then_inc(s_tab, 16)
            sp.wait_ge(s_cols, 1)
            sp.dma_start(pen_d, pen[0:NG, :]).then_inc(s_pen, 16)
            sp.wait_ge(s_pen, 16)
            sp.wait_ge(s_tab, 32)

        @block.gpsimd
        def _(pool):
            pool.memset(ident[:, :], 0.0).then_inc(s_id, 1)
            pool.wait_ge(s_id, 1)
            pool.affine_select(out=ident[:, :], in_=ident[:, :], compare_op=ALU.not_equal, fill=1.0,
                               base=0, pattern=[[-1, P]], channel_multiplier=1).then_inc(s_id, 1)
            pool.iota(keep["iotai"][:, :], pattern=[[1, ROWS]], base=0, channel_multiplier=0).then_inc(s_id, 1)

        @block.vector
        def _(v):
            v.memset(srci[:, :], 0).then_inc(s_clear, 1)
            v.memset(dsti[:, :], int(PAD_DST)).then_inc(s_clear, 1)
            v.memset(dirs[:, :, :], 0.0).then_inc(s_clear, 1)
            v.memset(empty[:, :, :], 0.0).then_inc(s_empty, 1)
            v.wait_ge(s_empty, 1)
            v.memset(empty[:, 1, 260:TABW], FAR).then_inc(s_empty, 1)
            v.memset(cut[:, 0:1], 0.0)
            v.memset(cut[:, ROWS:ROWS + 1], 0.0)
            v.wait_ge(s_id, 3)
            v.tensor_copy(keep["iota"][:, :], keep["iotai"][:, :])
            v.wait_ge(s_load, 96)
            v.tensor_copy(srcf[:, :], srci[:, :])
            v.tensor_copy(dstf[:, :], dsti[:, :]).then_inc(s_cut, 1)
            v.wait_ge(s_cut, 1)
            v.tensor_tensor(cut[:, 1:ROWS], dstf[:, 0:ROWS - 1], dstf[:, 1:ROWS], ALU.not_equal)
            v.tensor_scalar(dstc[:, :], dstf[:, :], float(N - 1), None, ALU.min).then_inc(s_cut, 1)
            v.wait_ge(s_cut, 2)
            v.tensor_scalar(pen[:, :], cut[:, :], FAR, None, ALU.mult)
            v.tensor_tensor_scan(rank[:, ::-1], cut[:, ROWS:0:-1], cut[:, ROWS:0:-1], 0.0, ALU.add, ALU.max)
            v.scalar_tensor_tensor(out=didx[:, :], in0=dstf[:, :], scalar=-PAD_DST, in1=cut[:, 1:ROWS + 1],
                                   op0=ALU.add, op1=ALU.mult).then_inc(s_cols, 1)
            for n, (_, _, out) in enumerate(jobs):
                v.wait_ge(s_tr, n + 1)
                v.tensor_copy(out, pt[n % 2][:, 0:4 * NG].rearrange("p (t g) -> p t g", t=4)).then_inc(s_ev, 1)
            v.wait_ge(s_tr, len(jobs) + 1)
            v.tensor_reduce(topf[:, 0:1], pt[0][0:1, 0:NG], AX.X, ALU.max).then_inc(s_top, 1)
            v.wait_ge(s_top, 1)
            v.tensor_copy(topi[:, :], topf[:, 0:1]).then_inc(s_top, 1)

        @block.tensor
        def _(pe):
            pe.wait_ge(s_id, 2)
            pe.wait_ge(s_cols, 1)
            for n, (a, half, _) in enumerate(jobs):
                at_least(pe, s_ev, n - 1)
                for t in range(4):
                    lo = (4 * half + t) * P
                    last = pe.transpose(pt[n % 2][:, t * NG:(t + 1) * NG], a[0:NG, lo:lo + P], ident[0:NG, 0:NG])
                last.then_inc(s_tr, 1)
            pe.wait_ge(s_ev, len(jobs))
            pe.transpose(pt[0][0:1, 0:NG], rank[0:NG, 0:1], ident[0:NG, 0:NG]).then_inc(s_tr, 1)


def norm_steps(v, i, b, x, st, mv, nrm, q):
    v.bn_stats(st[b][:, :], x).then_inc(q["stats"], 1)
    hold(v, q["stats"], i + 1, q["passed"])
    v.bn_aggr(mv[b][:, :], st[b][:, :]).then_inc(q["mv"], 1)
    v.wait_ge(q["root"], i + 1)
    v.reciprocal(nrm[b][:, 0:1], nrm[b][:, 2:3]).then_inc(q["recip"], 1)
    v.wait_ge(q["recip"], i + 1)
    v.scalar_tensor_tensor(out=nrm[b][:, 1:2], in0=mv[b][:, 0:1], scalar=-1.0, in1=nrm[b][:, 0:1],
                           op0=ALU.mult, op1=ALU.mult).then_inc(q["nrm"], 1)


def norm_relu(a, i, b, x, h, mv, nrm, eps, q):
    a.wait_ge(q["mv"], i + 1)
    a.activation(nrm[b][:, 2:3], mv[b][:, 1:2], ACT.Sqrt, bias=eps[:, 0:1]).then_inc(q["root"], 1)
    a.wait_ge(q["nrm"], i + 1)
    at_least(a, q["turned"], i - 1)
    a.activation(h[b][:, :], x, ACT.Relu, bias=nrm[b][:, 1:2], scale=nrm[b][:, 0:1]).then_inc(q["h"], 1)


def turn(pe, i, b, h, hps, ident, q):
    pe.wait_ge(q["h"], i + 1)
    at_least(pe, q["hT"], i - 1)
    for k in range(2):
        last = pe.transpose(hps[b][:, k * P:(k + 1) * P], h[b][:, k * P:(k + 1) * P], ident[:, :])
    last.then_inc(q["turned"], 1)


def project_nodes(nc, keep, x, Wq, bq, Wk, bk, Wv, bv, Ws, bs, q_d, kv_d, skip_d):
    with ExitStack() as ctx:
        m = Scope(nc, ctx)
        W = m.sb("Wqkvs", [P, 2, 4 * D])
        bias = m.sb("bias4", [P, 4 * D])
        xt = [m.sb(f"xt{b}", [P, D]) for b in range(2)]
        h = [m.sb(f"h{b}", [P, D]) for b in range(2)]
        hT = [m.sb(f"hT{b}", [P, D]) for b in range(2)]
        res = [m.sb(f"res{b}", [P, 4 * D]) for b in range(2)]
        st = [m.sb(f"st{b}", [P, 6]) for b in range(2)]
        mv = [m.sb(f"mv{b}", [P, 2]) for b in range(2)]
        nrm = [m.sb(f"nrm{b}", [P, 3]) for b in range(2)]
        eps = m.sb("eps", [P, 1])
        hps = [m.ps(f"hps{b}", [P, 512]) for b in range(2)]
        proj = [m.ps(f"proj{b}", [P, 4 * D]) for b in range(2)]
        q = {n: m.sem(f"n0_{n}") for n in ("passed", "stats", "mv", "root", "recip", "nrm", "h", "turned", "hT", "proj", "sum",
                                           "res", "w", "scaled", "eps")}
        s_x = [m.sem(f"n0_x{b}") for b in range(2)]
        s_out = [m.sem(f"n0_out{b}") for b in range(2)]
        ident = keep["ident"]
        block = ctx.enter_context(nc.Block())

        @block.sync
        def _(sp):
            for n, (w, b_) in enumerate(((Wq, bq), (Wk, bk), (Wv, bv), (Ws, bs))):
                sp.dma_start(W[:, :, n * D:(n + 1) * D], w.rearrange("(k p) n -> p k n", p=P)).then_inc(q["w"], 16)
                sp.dma_start(bias[:, n * D:(n + 1) * D],
                             b_.rearrange("(a n) -> a n", a=1).to_broadcast([P, D])).then_inc(q["w"], 16)

            def load(i, b):
                at_least(sp, q["res"], i - 1)
                if isinstance(i, int) and i == NT - 1:
                    sp.dma_start(xt[b][0:LAST_NODES, :], x[i * P:N, :]).then_inc(s_x[b], 16)
                else:
                    sp.dma_start(xt[b][:, :], x[bass.ds(i * P, P), :]).then_inc(s_x[b], 16)

            def store(i, b):
                sp.wait_ge(q["res"], i + 1)
                rows = bass.ds(i * P, P)
                sp.dma_start(q_d[rows, :], res[b][:, 0:D]).then_inc(s_out[b], 16)
                sp.dma_start(kv_d[rows, :], res[b][:, D:3 * D]).then_inc(s_out[b], 16)
                sp.dma_start(skip_d[rows, :], res[b][:, 3 * D:]).then_inc(s_out[b], 16)

            load(0, 0)
            load(1, 1)

            def both(i, b):
                store(i, b)
                if not isinstance(i, int) or i + 2 < NT:
                    load(i + 2, b)

            sweep(sp, both, 2, NT - 3, NT)
            for b in range(2):
                sp.wait_ge(s_out[b], 48 * ((NT + 1 - b) // 2))

        @block.vector
        def _(v):
            v.memset(eps[:, :], 1e-5).then_inc(q["eps"], 1)
            v.wait_ge(q["w"], 128)
            v.tensor_scalar(W[:, :, 0:D], W[:, :, 0:D], 32.0 ** -0.5, None, ALU.mult)
            v.tensor_scalar(bias[:, 0:D], bias[:, 0:D], 32.0 ** -0.5, None, ALU.mult).then_inc(q["scaled"], 1)
            v.wait_ge(q["scaled"], 1)

            def norm(i, b):
                v.wait_ge(s_x[b], uses(i, b, 16))
                norm_steps(v, i, b, xt[b][:, :], st, mv, nrm, q)

            def finish(i, b):
                v.wait_ge(q["proj"], i + 1)
                if not (isinstance(i, int) and i < 2):
                    v.wait_ge(s_out[b], uses(i, b, 48) - 48)
                for k in range(2):
                    last = v.tensor_tensor(res[b][:, k * 512:(k + 1) * 512], proj[b][:, k * 512:(k + 1) * 512],
                                           bias[:, k * 512:(k + 1) * 512], ALU.add)
                last.then_inc(q["sum"], 1)
                v.wait_ge(q["sum"], i + 1)
                v.tensor_tensor(res[b][:, 3 * D:], res[b][:, 3 * D:], xt[b][:, :], ALU.add).then_inc(q["res"], 1)

            def step(i, b):
                if not (isinstance(i, int) and i >= NT):
                    norm(i, b)
                if not (isinstance(i, int) and i < 1):
                    finish(i - 1, 1 - b)

            sweep(v, step, 4, NT - 1, NT + 1)

        @block.scalar
        def _(a):
            a.wait_ge(q["eps"], 1)

            def step(i, b):
                a.wait_ge(s_x[b], uses(i, b, 16))
                norm_relu(a, i, b, xt[b][:, :], h, mv, nrm, eps, q)
                a.wait_ge(q["turned"], i + 1)
                at_least(a, q["proj"], i - 1)
                a.activation(hT[b][:, :], hps[b][:, 0:D], ACT.Copy).then_inc(q["hT"], 1)

            sweep(a, step, 2, NT - 1, NT)

        @block.tensor
        def _(pe):
            pe.wait_ge(q["scaled"], 1)

            def step(i, b):
                turn(pe, i, b, h, hps, ident, q)
                pe.wait_ge(q["hT"], i + 1)
                at_least(pe, q["sum"], i - 1)
                for n in range(2):
                    for k in range(2):
                        last = pe.matmul(proj[b][:, n * 512:(n + 1) * 512], hT[b][:, k * P:(k + 1) * P],
                                         W[:, k, n * 512:(n + 1) * 512], start=(k == 0), stop=(k == 1))
                last.then_inc(q["proj"], 1)

            sweep(pe, step, 2, NT - 1, NT)


def edge_layer(nc, keep, layer, pen_d, tab, kv_d=None, q_d=None, edge_attr=None, We_d=None, fr_d=None):
    first = layer == 0
    H = 8 if first else 4
    C = D // 8 if first else 64
    PARTS = 4 if first else 2
    TP = G // PARTS
    FRW = 2 * (C + H)
    DEN = D
    with ExitStack() as ctx:
        m = Scope(nc, ctx)
        L = f"L{layer}_"
        two = range(2)
        if first:
            KV = [m.sb(f"{L}KV{b}", [P, G, 2 * D]) for b in two]
            Q = [m.sb(f"{L}Q{b}", [P, G, D]) for b in two]
            ea = [m.sb(f"{L}ea{b}", [P, G, D]) for b in two]
            eaT = [m.sb(f"{L}eaT{b}", [P, 4 * P]) for b in two]
            We = m.sb(f"{L}We", [P, 2, D])
            VAL = [m.sb(f"{L}VE{b}", [P, G, D]) for b in two]
            T = [m.ps(f"{L}T{b}", [P, 512]) for b in two]
            Ep = [m.ps(f"{L}E{b}", [P, 512]) for b in two]
        else:
            FR = [m.sb(f"{L}FR{b}", [P, G, FRW]) for b in two]
            VAL = [m.sb(f"{L}M{b}", [P, G, C + H]) for b in two]
        idx = [m.sb(f"{L}idx{b}", [P, G, 2], I32) for b in two]
        alpha = [m.sb(f"{L}alpha{b}", [P, G, H]) for b in two]
        pen = [m.sb(f"{L}pen{b}", [H, ROWS + 1]) for b in two]
        fwd = m.sb(f"{L}fwd", [H, ROWS])
        top = [m.sb(f"{L}top{b}", [H, ROWS]) for b in two]
        dif = [m.sb(f"{L}dif{b}", [H, ROWS + 1]) for b in two]
        far = m.sb(f"{L}far", [H, 1])
        wgt = [m.sb(f"{L}wgt{b}", [P, (G + 1) * H]) for b in two]
        msg = [m.sb(f"{L}msg{b}", [P, G, MSGW]) for b in two]
        mask = [m.sb(f"{L}mask{b}", [P, G, P]) for b in two]
        O = [m.sb(f"{L}O{b}", [P, TABW]) for b in two]
        node = [m.sb(f"{L}node{b}", [P, 1], I32) for b in two]
        opened = [m.sb(f"{L}open{b}", [1, DEN + H]) for b in two]
        carry = [m.sb(f"{L}carry{b}", [1, DEN + H]) for b in two]
        turned = m.ps(f"{L}aT", [P, ROWS])
        back = m.ps(f"{L}back", [P, 512])
        Op = m.ps(f"{L}Op", [P, 512])

        names = ["passed", "kj", "ve", "prod", "alpha", "fwd", "top", "dif", "aT", "back", "wgt", "row0", "den", "mx", "msg",
                 "mask", "carry", "sum", "rows", "idx", "t", "tT", "e", "scaled", "setup", "we"]
        s = {n: m.sem(L + n) for n in names}
        s_in = [[m.sem(f"{L}in{b}_{p}") for p in range(PARTS)] for b in two]
        s_ea = [m.sem(f"{L}ea_in{b}") for b in two]
        s_pen = [m.sem(f"{L}pen_in{b}") for b in two]
        s_put = [m.sem(f"{L}put{b}") for b in two]
        per_part = 16 * TP * (2 if first else 1)
        ident, metaf, metai, iota = keep["ident"], keep["metaf"], keep["metai"], keep["iota"]
        need_rounds = keep["top"]
        block = ctx.enter_context(nc.Block())

        def choose(eng, program):
            most = eng.value_load(need_rounds[0:1, 0:1])
            with eng.If(most < P):
                program(1)
            with eng.Else():
                program(ALL_ROUNDS)

        def live(i):
            return not isinstance(i, int) or 0 <= i < NG

        @block.sync
        def _(sp):
            if first:
                sp.dma_start(We[:, :, :], We_d.rearrange("(k p) n -> p k n", p=P)).then_inc(s["we"], 16)

            def step(i, b):
                if first:
                    at_least(sp, s["t"], 4 * (i - 1))
                    if isinstance(i, int) and i == NG - 1:
                        full = LAST_ROWS // P
                        lo = i * STEP
                        sp.dma_start(ea[b][:, 0:full, :], edge_attr[lo:lo + full * P, :].rearrange("(t p) d -> p t d", p=P)
                                     ).then_inc(s_ea[b], 16)
                        sp.dma_start(ea[b][0:LAST_ROWS % P, full, :], edge_attr[lo + full * P:E, :]).then_inc(s_ea[b], 16)
                    else:
                        sp.dma_start(ea[b][:, :, :], edge_attr[bass.ds(i * STEP, ROWS), :].rearrange(
                            "(t p) d -> p t d", p=P)).then_inc(s_ea[b], 16)
                at_least(sp, s["top"], i - 1)
                sp.dma_start(pen[b][:, :], pen_d[bass.ds(i, 1), :].to_broadcast([H, ROWS + 1])).then_inc(s_pen[b], 16)

            sweep(sp, step, 4, NG - 2, NG)

        @block.gpsimd
        def _(pool):
            def program(rounds):
                lag = 4 if rounds == 1 else 2

                def gather(i, b, p):
                    t0 = p * TP
                    hold(pool, s["alpha"], PARTS * (i - 2) + p + 1, s["passed"])
                    pool.tensor_copy(idx[b][:, t0:t0 + TP, :], metai[:, i, t0:t0 + TP, :]).then_inc(s["idx"], 1)
                    hold(pool, s["idx"], PARTS * i + p + 1, s["passed"])
                    for t in range(t0, t0 + TP):
                        if first:
                            pool.indirect_dma_start(out=KV[b][:, t, :], out_offset=None, in_=kv_d,
                                                    in_offset=bass.IndirectOffsetOnAxis(ap=idx[b][:, t, 0:1], axis=0)
                                                    ).then_inc(s_in[b][p], 16)
                            pool.indirect_dma_start(out=Q[b][:, t, :], out_offset=None, in_=q_d,
                                                    in_offset=bass.IndirectOffsetOnAxis(ap=idx[b][:, t, 1:2], axis=0)
                                                    ).then_inc(s_in[b][p], 16)
                        else:
                            pool.indirect_dma_start(out=FR[b][:, t, :], out_offset=None, in_=fr_d,
                                                    in_offset=bass.IndirectOffsetOnAxis(ap=idx[b][:, t, 0:1], axis=0)
                                                    ).then_inc(s_in[b][p], 16)

                def put(g, b):
                    for r in range(rounds):
                        c = b if rounds == 1 else r % 2
                        hold(pool, s["rows"], rounds * g + r + 1, s["passed"])
                        pool.indirect_dma_start(out=tab, out_offset=bass.IndirectOffsetOnAxis(ap=node[c][:, 0:1], axis=0),
                                                in_=O[c][:, :], in_offset=None, bounds_check=N - 1, oob_is_err=False
                                                ).then_inc(s_put[c], 16)

                def step(i, b):
                    for p in range(PARTS):
                        if live(i):
                            gather(i, b, p)
                        if p == PARTS // 2 - 1 and live(i - lag):
                            put(i - lag, b)

                sweep(pool, step, 4, NG - 2, NG + lag)
                for c in range(2):
                    pool.wait_ge(s_put[c], 16 * rounds * NG // 2)

            choose(pool, program)

        @block.tensor
        def _(pe):
            if first:
                pe.wait_ge(s["we"], 16)

            def program(rounds):
                def attr_turn(i, b, p):
                    n = 4 * i + p
                    if p == 0:
                        pe.wait_ge(s_ea[b], uses(i, b, 16) + (16 if isinstance(i, int) and i == NG - 1 else 0))
                    at_least(pe, s["tT"], n - 1)
                    for u in range(2):
                        for k in range(2):
                            last = pe.transpose(T[p % 2][:, (2 * u + k) * P:(2 * u + k + 1) * P],
                                                ea[b][:, 2 * p + u, k * P:(k + 1) * P], ident[:, :])
                    last.then_inc(s["t"], 1)

                def attr_project(i, b, p):
                    n = 4 * i + p
                    pe.wait_ge(s["tT"], n + 1)
                    at_least(pe, s["ve"], n - 1)
                    for u in range(2):
                        for k in range(2):
                            last = pe.matmul(Ep[p % 2][:, u * D:(u + 1) * D], eaT[p % 2][:, (2 * u + k) * P:(2 * u + k + 1) * P],
                                             We[:, k, :], start=(k == 0), stop=(k == 1))
                    last.then_inc(s["e"], 1)

                def attrs(i, b, p):
                    if not first or not live(i):
                        return
                    if p < 3:
                        attr_turn(i, b, p + 1)
                    elif live(i + 1):
                        attr_turn(i + 1, 1 - b, 0)
                    attr_project(i, b, p)

                def scores_turn(g, b):
                    pe.wait_ge(s["alpha"], PARTS * (g + 1))
                    at_least(pe, s["dif"], g)
                    for t in range(G):
                        last = pe.transpose(turned[0:H, t * P:(t + 1) * P], alpha[b][:, t, :], ident[:, :])
                    last.then_inc(s["aT"], 1)

                def scores_back(g, b):
                    hold(pe, s["wgt"] if first else s["mx"], g, s["passed"])
                    hold(pe, s["dif"], g + 1, s["passed"])
                    for t in range(G):
                        pe.transpose(back[:, t * H:(t + 1) * H], dif[b][:, t * P:(t + 1) * P], ident[0:H, 0:H])
                    pe.transpose(back[0:1, G * H:(G + 1) * H], dif[b][:, ROWS:ROWS + 1], ident[0:H, 0:H]
                                 ).then_inc(s["back"], 1)

                def run_sums(g, b):
                    pe.wait_ge(s["msg"], g + 1)
                    pe.wait_ge(s["den"], g + 1)
                    for r in range(rounds):
                        c = b if rounds == 1 else r % 2
                        pe.wait_ge(s["mask"], rounds * g + r + 1)
                        at_least(pe, s["rows"], rounds * g + r)
                        for t in range(G):
                            last = pe.matmul(Op[:, 0:MSGW], mask[c][:, t, :], msg[b][:, t, :], start=(t == 0),
                                             stop=(t == G - 1))
                            if t == 0 and not (isinstance(g, int) and g == 0):
                                pe.wait_ge(s["carry"], g)
                                pe.matmul(Op[:, 0:DEN + H], mask[c][0:1, 0, :], carry[b][:, :], start=False, stop=False)
                        last.then_inc(s["sum"], 1)

                def step(i, b):
                    attrs(i, b, 0)
                    if live(i - 1):
                        scores_turn(i - 1, 1 - b)
                    attrs(i, b, 1)
                    if live(i - 2):
                        run_sums(i - 2, b)
                    attrs(i, b, 2)
                    if live(i - 1):
                        scores_back(i - 1, 1 - b)
                    attrs(i, b, 3)

                if first:
                    attr_turn(0, 0, 0)
                sweep(pe, step, 4, NG - 2, NG + 2)

            choose(pe, program)

        @block.scalar
        def _(a):
            def program(rounds):
                def attr_copy(i, b, p):
                    n = 4 * i + p
                    a.wait_ge(s["t"], n + 1)
                    at_least(a, s["e"], n - 1)
                    a.activation(eaT[p % 2][:, :], T[p % 2][:, :], ACT.Copy).then_inc(s["tT"], 1)

                def weights(g, b):
                    a.wait_ge(s["back"], g + 1)
                    at_least(a, s["msg"], g - 1)
                    at_least(a, s["carry"], g - 2)
                    a.activation(wgt[b][:, 0:G * H], back[:, 0:G * H], ACT.Exp)
                    a.activation(wgt[b][0:1, G * H:], back[0:1, G * H:(G + 1) * H], ACT.Exp).then_inc(s["wgt"], 1)

                def side_columns(g, b):
                    at_least(a, s["sum"], rounds * (g - 1))
                    a.activation(msg[b][:, :, TABW:MSGW], metaf[:, g, DIDX * G:(DIDX + 1) * G].unsqueeze(2), ACT.Copy)
                    a.wait_ge(s["wgt"], g + 1)
                    at_least(a, s["row0"], g)
                    a.activation(msg[b][:, :, DEN:DEN + H], wgt[b][:, 0:G * H].rearrange("p (t h) -> p t h", h=H),
                                 ACT.Copy).then_inc(s["den"], 1)

                def rows(g, b):
                    for r in range(rounds):
                        c = b if rounds == 1 else r % 2
                        n = rounds * g + r
                        a.wait_ge(s["sum"], n + 1)
                        if rounds == 1:
                            if not (isinstance(g, int) and g < 2):
                                a.wait_ge(s_put[c], uses(g, b, 16) - 16)
                        else:
                            at_least(a, s_put[c], 16 * (4 * g + r // 2))
                        if r == 0:
                            at_least(a, s["carry"], g - 1)
                            a.activation(opened[b][:, :], Op[0:1, 0:DEN + H], ACT.Copy)
                        a.activation(node[c][:, :], Op[:, TABW:MSGW], ACT.Copy, bias=PAD_DST)
                        a.activation(O[c][:, :], Op[:, 0:TABW], ACT.Copy).then_inc(s["rows"], 1)

                def step(i, b):
                    if first and live(i):
                        attr_copy(i, b, 0)
                        attr_copy(i, b, 1)
                    if live(i - 2):
                        rows(i - 2, b)
                    if first and live(i):
                        attr_copy(i, b, 2)
                    if live(i - 1):
                        weights(i - 1, 1 - b)
                    if first and live(i):
                        attr_copy(i, b, 3)
                    if live(i - 1):
                        side_columns(i - 1, 1 - b)

                sweep(a, step, 4, NG - 2, NG + 2)

            if first:
                assert DEN + H == TABW
            choose(a, program)

        @block.vector
        def _(v):
            v.memset(far[:, :], FAR).then_inc(s["setup"], 1)
            v.wait_ge(s["setup"], 1)

            def program(rounds):
                def form0(i, b, p):
                    n, ts = 4 * i + p, slice(2 * p, 2 * p + 2)
                    e = Ep[p % 2][:, :].rearrange("p (t d) -> p t d", t=2)
                    v.wait_ge(s["e"], n + 1)
                    v.wait_ge(s_in[b][p], uses(i, b, per_part))
                    v.tensor_tensor(KV[b][:, ts, 0:D], KV[b][:, ts, 0:D], e, ALU.add).then_inc(s["kj"], 1)
                    at_least(v, s["msg"], i - 1)
                    v.tensor_tensor(VAL[b][:, ts, :], KV[b][:, ts, D:], e, ALU.add).then_inc(s["ve"], 1)
                    v.wait_ge(s["kj"], n + 1)
                    v.tensor_tensor(Q[b][:, ts, :], Q[b][:, ts, :], KV[b][:, ts, 0:D], ALU.mult).then_inc(s["prod"], 1)
                    v.wait_ge(s["prod"], n + 1)
                    at_least(v, s["aT"], i - 1)
                    v.tensor_reduce(alpha[b][:, ts, :], Q[b][:, ts, :].rearrange("p t (h c) -> p t h c", c=C),
                                    AX.X, ALU.add).then_inc(s["alpha"], 1)

                def form1(i, b, p):
                    n, ts, w = 2 * i + p, slice(p * TP, p * TP + TP), C + H
                    v.wait_ge(s_in[b][p], uses(i, b, per_part))
                    for k, d in enumerate((DIR0, DIR1)):
                        part = FR[b][:, ts, k * w:(k + 1) * w]
                        amount = metaf[:, i, d * G + p * TP:d * G + p * TP + TP].unsqueeze(2).to_broadcast([P, TP, w])
                        last = v.tensor_tensor(part, part, amount, ALU.mult)
                    last.then_inc(s["prod"], 1)
                    v.wait_ge(s["prod"], n + 1)
                    at_least(v, s["msg"], i - 1)
                    v.tensor_tensor(VAL[b][:, ts, :], FR[b][:, ts, 0:w], FR[b][:, ts, w:], ALU.add).then_inc(s["ve"], 1)
                    v.wait_ge(s["ve"], n + 1)
                    at_least(v, s["aT"], i - 1)
                    at_least(v, s["mx"], i - 1)
                    sc = VAL[b][:, ts, C:]
                    v.scalar_tensor_tensor(out=alpha[b][:, ts, :], in0=sc, scalar=0.2, in1=sc, op0=ALU.mult,
                                           op1=ALU.max).then_inc(s["alpha"], 1)

                def scans(g, b):
                    before = far[:, 0:1] if isinstance(g, int) and g == 0 else top[1 - b][:, STEP:ROWS]
                    v.wait_ge(s_pen[b], uses(g, b, 16))
                    v.wait_ge(s["aT"], g + 1)
                    at_least(v, s["top"], g)
                    v.tensor_tensor_scan(fwd[:, :], pen[b][:, 0:ROWS], turned[0:H, :], before, ALU.add, ALU.max
                                         ).then_inc(s["fwd"], 1)
                    v.wait_ge(s["fwd"], g + 1)
                    v.tensor_tensor_scan(top[b][:, ::-1], pen[b][:, ROWS:0:-1], fwd[:, ::-1], FAR, ALU.add, ALU.max
                                         ).then_inc(s["top"], 1)
                    v.wait_ge(s["top"], g + 1)
                    at_least(v, s["back"], g - 1)
                    v.tensor_tensor(dif[b][:, ROWS:ROWS + 1], before, top[b][:, 0:1], ALU.subtract)
                    v.tensor_tensor(dif[b][:, 0:ROWS], turned[0:H, :], top[b][:, :], ALU.subtract).then_inc(s["dif"], 1)

                def masks(g, b):
                    for r in range(rounds):
                        c = b if rounds == 1 else r % 2
                        n = rounds * g + r
                        at_least(v, s["sum"], n - 1)
                        for t in range(G):
                            last = v.tensor_scalar(mask[c][:, t, :], iota[:, r * P:(r + 1) * P],
                                                   metaf[:, g, RANK * G + t:RANK * G + t + 1], None, ALU.is_equal)
                        last.then_inc(s["mask"], 1)

                def carried(g, b):
                    if isinstance(g, int) and g == 0:
                        return
                    v.wait_ge(s["rows"], rounds * (g - 1) + 1)
                    v.wait_ge(s["wgt"], g + 1)
                    at_least(v, s["sum"], rounds * (g - 1))
                    f = wgt[b][0:1, G * H:(G + 1) * H]
                    v.tensor_tensor(carry[b][:, 0:DEN].rearrange("p (h c) -> p h c", c=C),
                                    opened[1 - b][:, 0:DEN].rearrange("p (h c) -> p h c", c=C),
                                    f.unsqueeze(2).to_broadcast([1, H, C]), ALU.mult)
                    v.tensor_tensor(carry[b][:, DEN:], opened[1 - b][:, DEN:], f, ALU.mult).then_inc(s["carry"], 1)

                def messages(g, b):
                    v.wait_ge(s["wgt"], g + 1)
                    if not (isinstance(g, int) and g == 0):
                        v.memset(wgt[b][0:1, 0:H], 0.0).then_inc(s["row0"], 1)
                        v.wait_ge(s["row0"], g)
                    at_least(v, s["sum"], rounds * (g - 1))
                    w4 = wgt[b][:, 0:G * H].rearrange("p (t h) -> p t h", h=H).unsqueeze(3).to_broadcast([P, G, H, C])
                    v.wait_ge(s["ve"], PARTS * (g + 1))
                    if first:
                        val = VAL[b][:, :, :].rearrange("p t (h c) -> p t h c", c=C)
                    else:
                        val = VAL[b][:, :, 0:C].unsqueeze(2).to_broadcast([P, G, H, C])
                        ends = metaf[:, g, END * G:(END + 1) * G].unsqueeze(2).to_broadcast([P, G, H])
                        mx = msg[b][:, :, DEN + H:DEN + 2 * H]
                        v.tensor_tensor(mx, alpha[b][:, :, :], back[:, 0:G * H].rearrange("p (t h) -> p t h", h=H),
                                        ALU.subtract).then_inc(s["mx"], 1)
                        v.wait_ge(s["mx"], g + 1)
                        v.tensor_tensor(mx, mx, ends, ALU.mult)
                    v.tensor_tensor(msg[b][:, :, 0:DEN].rearrange("p t (h c) -> p t h c", c=C), val, w4, ALU.mult
                                    ).then_inc(s["msg"], 1)

                form = form0 if first else form1

                def step(i, b):
                    at = 0
                    def parts(n):
                        nonlocal at
                        for p in range(at, min(at + n, PARTS)):
                            if live(i):
                                form(i, b, p)
                        at += n
                    parts(1)
                    if live(i - 2):
                        masks(i - 2, b)
                        carried(i - 2, b)
                    parts(1 if first else 0)
                    if live(i - 1):
                        scans(i - 1, 1 - b)
                    parts(PARTS)
                    if live(i - 1):
                        messages(i - 1, 1 - b)

                sweep(v, step, 4, NG - 2, NG + 2)

            choose(v, program)


def between(nc, keep, skip_d, tab0, Wf, Wr, attn, x1_d, fr_d):
    H, C = 8, 32
    F, H1 = 64, 4
    FW = F + H1
    with ExitStack() as ctx:
        m = Scope(nc, ctx)
        two = range(2)
        wrows = m.sb("wrows", [F, 2, D])
        arow = m.sb("arow", [H1, F])
        acol = m.sb("acol", [F, H1])
        W = m.sb("Wfr", [P, 2, 2 * FW])
        A = [m.sb(f"b_A{b}", [P, TABW]) for b in two]
        X = [m.sb(f"b_X{b}", [P, D]) for b in two]
        h = [m.sb(f"b_h{b}", [P, D]) for b in two]
        hT = [m.sb(f"b_hT{b}", [P, D]) for b in two]
        den = [m.sb(f"b_den{b}", [P, H]) for b in two]
        fr = [m.sb(f"b_fr{b}", [P, 2 * FW]) for b in two]
        st = [m.sb(f"b_st{b}", [P, 6]) for b in two]
        mv = [m.sb(f"b_mv{b}", [P, 2]) for b in two]
        nrm = [m.sb(f"b_nrm{b}", [P, 3]) for b in two]
        eps = m.sb("b_eps", [P, 1])
        hps = [m.ps(f"b_hps{b}", [P, 512]) for b in two]
        proj = [m.ps(f"b_proj{b}", [P, 512]) for b in two]
        wps = m.ps("wps", [P, 512])
        q = {n: m.sem(f"n1_{n}") for n in ("passed", "stats", "mv", "root", "recip", "nrm", "h", "turned", "hT", "proj", "fr",
                                           "w", "eps", "den", "inv", "scaled", "x1", "prep", "preped")}
        s_in = [m.sem(f"n1_in{b}") for b in two]
        s_x1 = [m.sem(f"n1_x1{b}") for b in two]
        s_fr = [m.sem(f"n1_frout{b}") for b in two]
        ident = keep["ident"]
        block = ctx.enter_context(nc.Block())

        @block.sync
        def _(sp):
            for n, w in enumerate((Wf, Wr)):
                sp.dma_start(wrows[:, n, :], w).then_inc(q["w"], 16)
            sp.dma_start(arow[:, :], attn.rearrange("a h f -> (a h) f")).then_inc(q["w"], 16)

            def load(i, b):
                at_least(sp, q["h"], i - 1)
                if not (isinstance(i, int) and i < 2):
                    sp.wait_ge(s_x1[b], uses(i, b, 16) - 16)
                sp.dma_start(A[b][:, :], tab0[bass.ds(i * P, P), :]).then_inc(s_in[b], 16)
                sp.dma_start(X[b][:, :], skip_d[bass.ds(i * P, P), :]).then_inc(s_in[b], 16)

            def store(i, b):
                sp.wait_ge(q["x1"], i + 1)
                sp.dma_start(x1_d[bass.ds(i * P, P), :], X[b][:, :]).then_inc(s_x1[b], 16)
                sp.wait_ge(q["fr"], i + 1)
                sp.dma_start(fr_d[bass.ds(i * P, P), :], fr[b][:, :]).then_inc(s_fr[b], 16)

            load(0, 0)
            load(1, 1)

            def both(i, b):
                store(i, b)
                if not isinstance(i, int) or i + 2 < NT:
                    load(i + 2, b)

            sweep(sp, both, 2, NT - 3, NT)
            for b in two:
                sp.wait_ge(s_x1[b], 16 * ((NT + 1 - b) // 2))
                sp.wait_ge(s_fr[b], 16 * ((NT + 1 - b) // 2))

        @block.vector
        def _(v):
            v.memset(eps[:, :], 1e-5).then_inc(q["eps"], 1)
            v.wait_ge(q["prep"], 1)
            v.tensor_copy(acol[:, :], wps[0:F, 0:H1]).then_inc(q["preped"], 1)
            v.wait_ge(q["prep"], 2)
            v.tensor_copy(W[:, :, :].rearrange("p k n -> p (k n)"), wps[:, 0:4 * FW]).then_inc(q["preped"], 1)

            def step(i, b):
                v.wait_ge(s_in[b], uses(i, b, 32))
                v.tensor_scalar(den[b][:, :], A[b][:, D:D + H], 1e-16, None, ALU.add).then_inc(q["den"], 1)
                v.wait_ge(q["den"], i + 1)
                v.reciprocal(den[b][:, :], den[b][:, :]).then_inc(q["inv"], 1)
                v.wait_ge(q["inv"], i + 1)
                acc = A[b][:, 0:D].rearrange("p (h c) -> p h c", c=C)
                v.tensor_tensor(acc, acc, den[b][:, :].unsqueeze(2).to_broadcast([P, H, C]), ALU.mult
                                ).then_inc(q["scaled"], 1)
                v.wait_ge(q["scaled"], i + 1)
                v.tensor_tensor(X[b][:, :], X[b][:, :], A[b][:, 0:D], ALU.add).then_inc(q["x1"], 1)
                v.wait_ge(q["x1"], i + 1)
                norm_steps(v, i, b, X[b][:, :], st, mv, nrm, q)

            sweep(v, step, 2, NT - 1, NT)

        @block.scalar
        def _(a):
            a.wait_ge(q["eps"], 1)

            def step(i, b):
                norm_relu(a, i, b, X[b][:, :], h, mv, nrm, eps, q)
                a.wait_ge(q["turned"], i + 1)
                at_least(a, q["proj"], i - 1)
                a.activation(hT[b][:, :], hps[b][:, 0:D], ACT.Copy).then_inc(q["hT"], 1)
                a.wait_ge(q["proj"], i + 1)
                if not (isinstance(i, int) and i < 2):
                    a.wait_ge(s_fr[b], uses(i, b, 16) - 16)
                a.activation(fr[b][:, :], proj[b][:, 0:2 * FW], ACT.Copy).then_inc(q["fr"], 1)

            sweep(a, step, 2, NT - 1, NT)

        @block.tensor
        def _(pe):
            pe.wait_ge(q["w"], 48)
            pe.transpose(wps[0:F, 0:H1], arow[:, :], ident[0:H1, 0:H1]).then_inc(q["prep"], 1)
            pe.wait_ge(q["preped"], 1)
            for k in range(2):
                for n in range(2):
                    at = (2 * k + n) * FW
                    half = wrows[:, n, k * P:(k + 1) * P]
                    pe.transpose(wps[:, at:at + F], half, ident[0:F, 0:F])
                    last = pe.matmul(wps[:, at + F:at + FW], half, acol[:, :], start=True, stop=True)
            last.then_inc(q["prep"], 1)
            pe.wait_ge(q["preped"], 2)

            def step(i, b):
                turn(pe, i, b, h, hps, ident, q)
                pe.wait_ge(q["hT"], i + 1)
                at_least(pe, q["fr"], i - 1)
                for k in range(2):
                    last = pe.matmul(proj[b][:, 0:2 * FW], hT[b][:, k * P:(k + 1) * P], W[:, k, :],
                                     start=(k == 0), stop=(k == 1))
                last.then_inc(q["proj"], 1)

            sweep(pe, step, 2, NT - 1, NT)


def finish(nc, keep, x1_d, tab1, out):
    H, C = 4, 64
    with ExitStack() as ctx:
        m = Scope(nc, ctx)
        two = range(2)
        MX = m.sb("f_MX", [P, NT, H])
        mcol = m.sb("f_mcol", [P, H])
        grow = m.sb("f_grow", [H, 1])
        diag = m.sb("f_diag", [H, H])
        ones = m.sb("f_ones", [H, P])
        gmax = m.sb("f_gmax", [P, H])
        A = [m.sb(f"f_A{b}", [P, TABW]) for b in two]
        X = [m.sb(f"f_X{b}", [P, D]) for b in two]
        R = [m.sb(f"f_R{b}", [P, D]) for b in two]
        w = [m.sb(f"f_w{b}", [P, H]) for b in two]
        f = [m.sb(f"f_f{b}", [P, H]) for b in two]
        ps = m.ps("f_ps", [P, 512])
        q = {n: m.sem(f"n2_{n}") for n in ("mx", "col", "colT", "row", "diag", "g", "gm", "ones", "sub", "exp", "den",
                                           "eps", "inv", "fac", "prod", "res")}
        s_in = [m.sem(f"n2_in{b}") for b in two]
        s_out = [m.sem(f"n2_out{b}") for b in two]
        ident = keep["ident"]
        block = ctx.enter_context(nc.Block())

        @block.sync
        def _(sp):
            with nc.allow_non_contiguous_dma(reason="four maxima per node"):
                sp.dma_start(MX[:, :, :], tab1[:, 260:TABW].rearrange("(t p) h -> p t h", p=P)).then_inc(q["mx"], 16)

            def load(i, b):
                at_least(sp, q["res"], i - 1)
                sp.dma_start(A[b][:, :], tab1[bass.ds(i * P, P), :]).then_inc(s_in[b], 16)
                sp.dma_start(X[b][:, :], x1_d[bass.ds(i * P, P), :]).then_inc(s_in[b], 16)

            def store(i, b):
                sp.wait_ge(q["res"], i + 1)
                if isinstance(i, int) and i == NT - 1:
                    sp.dma_start(out[i * P:N, :], R[b][0:LAST_NODES, :]).then_inc(s_out[b], 16)
                else:
                    sp.dma_start(out[bass.ds(i * P, P), :], R[b][:, :]).then_inc(s_out[b], 16)

            load(0, 0)
            load(1, 1)

            def both(i, b):
                store(i, b)
                if not isinstance(i, int) or i + 2 < NT:
                    load(i + 2, b)

            sweep(sp, both, 2, NT - 3, NT)
            for b in two:
                sp.wait_ge(s_out[b], 16 * ((NT + 1 - b) // 2))

        @block.tensor
        def _(pe):
            pe.wait_ge(q["col"], 1)
            pe.transpose(ps[0:H, 0:P], mcol[:, :], ident[:, :]).then_inc(q["colT"], 1)
            pe.wait_ge(q["diag"], 1)
            pe.matmul(ps[:, P:P + H], ones[:, :], diag[:, :], start=True, stop=True).then_inc(q["g"], 1)

        @block.vector
        def _(v):
            v.memset(ones[:, :], 1.0).then_inc(q["ones"], 1)
            v.wait_ge(q["mx"], 16)
            v.tensor_reduce(mcol[:, :], MX[:, :, :].rearrange("p t h -> p h t"), AX.X, ALU.max).then_inc(q["col"], 1)
            v.wait_ge(q["colT"], 1)
            v.tensor_reduce(grow[:, :], ps[0:H, 0:P], AX.X, ALU.max).then_inc(q["row"], 1)
            v.wait_ge(q["row"], 1)
            v.tensor_scalar(diag[:, :], ident[0:H, 0:H], grow[:, 0:1], None, ALU.mult).then_inc(q["diag"], 1)
            v.wait_ge(q["g"], 1)
            v.tensor_copy(gmax[:, :], ps[:, P:P + H]).then_inc(q["gm"], 1)
            v.wait_ge(q["gm"], 1)

            def step(i, b):
                v.wait_ge(s_in[b], uses(i, b, 32))
                v.tensor_tensor(w[b][:, :], A[b][:, 260:TABW], gmax[:, :], ALU.subtract).then_inc(q["sub"], 1)
                v.wait_ge(q["exp"], i + 1)
                v.tensor_tensor(f[b][:, :], A[b][:, D:D + H], w[b][:, :], ALU.mult).then_inc(q["den"], 1)
                v.wait_ge(q["den"], i + 1)
                v.tensor_scalar(f[b][:, :], f[b][:, :], 1e-10, None, ALU.add).then_inc(q["eps"], 1)
                v.wait_ge(q["eps"], i + 1)
                v.reciprocal(f[b][:, :], f[b][:, :]).then_inc(q["inv"], 1)
                v.wait_ge(q["inv"], i + 1)
                v.tensor_tensor(f[b][:, :], f[b][:, :], w[b][:, :], ALU.mult).then_inc(q["fac"], 1)
                v.wait_ge(q["fac"], i + 1)
                if not (isinstance(i, int) and i < 2):
                    v.wait_ge(s_out[b], uses(i, b, 16) - 16)
                v.tensor_tensor(R[b][:, :].rearrange("p (h c) -> p h c", c=C), A[b][:, 0:D].rearrange(
                    "p (h c) -> p h c", c=C), f[b][:, :].unsqueeze(2).to_broadcast([P, H, C]), ALU.mult
                                ).then_inc(q["prod"], 1)
                v.wait_ge(q["prod"], i + 1)
                v.tensor_tensor(R[b][:, :], R[b][:, :], X[b][:, :], ALU.add).then_inc(q["res"], 1)

            sweep(v, step, 2, NT - 1, NT)

        @block.scalar
        def _(a):
            def step(i, b):
                a.wait_ge(q["sub"], i + 1)
                a.activation(w[b][:, :], w[b][:, :], ACT.Exp).then_inc(q["exp"], 1)

            sweep(a, step, 2, NT - 1, NT)


def build(nc, x, src, dst, edge_attr_2, edge_attr_256, Wq, bq, Wk, bk, Wv, bv, We, Ws, bs, Wf, Wr, attn, out):
    def scratch(name, shape):
        return nc.dram_tensor(name, shape, F32, kind="Internal").ap()

    q_d, kv_d, skip_d = scratch("q_d", [NPAD, D]), scratch("kv_d", [NPAD, 2 * D]), scratch("skip_d", [NPAD, D])
    x1_d, fr_d = scratch("x1_d", [NPAD, D]), scratch("fr_d", [NPAD, 136])
    tab0, tab1 = scratch("tab0", [NPAD, TABW]), scratch("tab1", [NPAD, TABW])
    pen_d = scratch("pen_d", [NG, ROWS + 1])
    with ExitStack() as ctx:
        m = Scope(nc, ctx)
        keep = {
            "ident": m.sb("ident", [P, P]),
            "iotai": m.sb("iotai", [P, ROWS], I32),
            "iota": m.sb("iota", [P, ROWS]),
            "metaf": m.sb("metaf", [P, NG, NF * G]),
            "metai": m.sb("metai", [P, NG, G, 2], I32),
            "top": m.sb("most_runs", [1, 1], I32),
        }
        prepare_edges(nc, keep, src, dst, edge_attr_2, pen_d, tab0, tab1)
        project_nodes(nc, keep, x, Wq, bq, Wk, bk, Wv, bv, Ws, bs, q_d, kv_d, skip_d)
        edge_layer(nc, keep, 0, pen_d, tab0, kv_d=kv_d, q_d=q_d, edge_attr=edge_attr_256, We_d=We)
        between(nc, keep, skip_d, tab0, Wf, Wr, attn, x1_d, fr_d)
        edge_layer(nc, keep, 1, pen_d, tab1, fr_d=fr_d)
        finish(nc, keep, x1_d, tab1, out)


_INS = ["x", "src", "dst", "edge_attr_2", "edge_attr_256", "L0_gnn_Wq", "L0_gnn_bq", "L0_gnn_Wk", "L0_gnn_bk",
        "L0_gnn_Wv", "L0_gnn_bv", "L0_gnn_We", "L0_gnn_Ws", "L0_gnn_bs", "L1_gnn_W_forward", "L1_gnn_W_reverse",
        "L1_gnn_attn_forward"]


def kernel(**inputs):
    import numpy as _np
    import concourse.bacc as _bacc
    from concourse import mybir as _mybir
    from concourse.bass_utils import run_bass_kernel_spmd as _run

    nc = _bacc.Bacc("TRN2", target_bir_lowering=False, num_devices=1)
    arrays, args = {}, []
    for name in _INS:
        a = _np.ascontiguousarray(inputs[name])
        arrays[f"in_{name}_dram"] = a
        args.append(nc.dram_tensor(f"in_{name}_dram", a.shape, _mybir.dt.from_np(a.dtype), kind="ExternalInput").ap())
    args.append(nc.dram_tensor("out_0_dram", [N, D], F32, kind="ExternalOutput").ap())
    build(nc, *args)
    r = _run(nc, [arrays], core_ids=[0])
    return r.results[0]["out_0_dram"]
```

```python
from contextlib import ExitStack

import concourse.bass as bass
from concourse import mybir

P = 128
N, E, D = 6250, 106250, 256
NT = (N + P - 1) // P
NPAD = NT * P
LAST_NODES = N - (NT - 1) * P
G = 8
ROWS = G * P
STEP = ROWS - 1
NG = (E - 1 + STEP - 1) // STEP
LAST_ROWS = E - (NG - 1) * STEP
PAD_DST = 8191.0
FAR = -1e38
TABW = 264
MSGW = TABW + 1
ALL_ROUNDS = ROWS // P
assert NG <= P and LAST_ROWS < ROWS and NG % 2 == 0

NRANK, DIDX, END, DIR0, DIR1 = range(5)
NF = 5

ALU = mybir.AluOpType
ACT = mybir.ActivationFunctionType
AX = mybir.AxisListType
F32 = mybir.dt.float32
I32 = mybir.dt.int32


def at_least(eng, sem, value):
    if isinstance(value, int) and value <= 0:
        return
    eng.wait_ge(sem, value)


def hold(eng, sem, value, passed):
    at_least(eng, sem, value)
    if not isinstance(value, int):
        eng.sem_inc(passed, 1)


def sweep(eng, body, first, last, stop, ways=2):
    for i in range(first):
        body(i, i % ways)
    with eng.Fori(first // ways, last // ways) as turn_:
        for k in range(ways):
            body(turn_ * ways + k, k)
    for i in range(last, stop):
        body(i, i % ways)


def uses(g, buf, per_use, ways=2):
    return (g - buf) * (per_use // ways) + per_use


class Scope:

    def __init__(self, nc, ctx):
        self.nc, self.ctx = nc, ctx

    def sb(self, name, shape, dt=F32):
        return self.ctx.enter_context(self.nc.sbuf_tensor(name, shape, dt))

    def ps(self, name, shape):
        return self.ctx.enter_context(self.nc.psum_tensor(name, shape, F32))

    def sem(self, name):
        return self.ctx.enter_context(self.nc.semaphore(name))


def prepare_edges(nc, keep, nodes, x, weights, src, dst, edge_attr_2, pen_d, tab0, tab1):
    with ExitStack() as ctx:
        m = Scope(nc, ctx)
        srci, dsti = m.sb("srci", [P, ROWS], I32), m.sb("dsti", [P, ROWS], I32)
        srcf, dstf, dstc = m.sb("srcf", [P, ROWS]), m.sb("dstf", [P, ROWS]), m.sb("dstc", [P, ROWS])
        dirs = m.sb("dirs", [P, ROWS, 2])
        cut = m.sb("cut", [P, ROWS + 1])
        pen, empty = nodes["pen"], nodes["empty"]
        rank, nrank, didx = m.sb("rank", [P, ROWS]), m.sb("nrank", [P, ROWS]), m.sb("didx", [P, ROWS])
        topf, topi = m.sb("topf", [1, 2]), keep["top"]
        pt = [m.ps(f"pt{b}", [P, 512]) for b in range(2)]
        s_clear, s_load, s_cols = m.sem("s_clear"), m.sem("s_load"), m.sem("s_cols")
        s_cut, s_id, s_tr, s_ev = m.sem("s_cut"), m.sem("s_id"), m.sem("s_tr"), m.sem("s_ev")
        s_top, s_empty = m.sem("s_top"), m.sem("s_empty")
        ident, metaf, metai = keep["ident"], keep["metaf"], keep["metai"]

        floats = {NRANK: nrank[:, :], DIDX: didx[:, :], END: cut[:, 1:ROWS + 1],
                  DIR0: dirs[:, :, 0], DIR1: dirs[:, :, 1]}
        jobs = []
        for half in range(2):
            for k, a in floats.items():
                out = metaf[:, :, k * G + 4 * half:k * G + 4 * half + 4].rearrange("p g t -> p t g")
                jobs.append((a, half, out))
            for k, a in ((0, srcf[:, :]), (1, dstc[:, :])):
                out = metai[:, :, 4 * half:4 * half + 4, k].rearrange("p g t -> p t g")
                jobs.append((a, half, out))
        block = ctx.enter_context(nc.Block())

        @block.sync
        def _(sp):
            sp.wait_ge(s_clear, 3)
            for flat, tile, w in ((src, srci[:, :], 1), (dst, dsti[:, :], 1),
                                  (edge_attr_2.rearrange("e c -> (e c)"), dirs[:, :, :].rearrange("p r c -> p (r c)"), 2)):
                rows = bass.AP(tensor=flat.tensor, offset=0, ap=[[STEP * w, NG - 1], [1, ROWS * w]])
                sp.dma_start(tile[0:NG - 1, :], rows).then_inc(s_load, 16)
                tail = flat[(NG - 1) * STEP * w:E * w].rearrange("(a b) -> a b", a=1)
                sp.dma_start(tile[NG - 1:NG, 0:LAST_ROWS * w], tail).then_inc(s_load, 16)
            sp.wait_ge(s_clear, 4)
            sp.dma_start(nodes["x"][:, 0:NT - 1, :], x[0:(NT - 1) * P, :].rearrange("(t p) d -> p t d", p=P)
                         ).then_inc(nodes["loaded"], 16)
            sp.dma_start(nodes["x"][0:LAST_NODES, NT - 1, :], x[(NT - 1) * P:N, :]).then_inc(nodes["loaded"], 16)
            for n, (w, b) in enumerate(weights):
                cols = slice(n * D, (n + 1) * D)
                sp.dma_start(nodes["W"][:, :, cols], w.rearrange("(k p) n -> p k n", p=P)).then_inc(nodes["w"], 16)
                sp.dma_start(nodes["bias"][:, cols], b.rearrange("(a n) -> a n", a=1).to_broadcast([P, D])
                             ).then_inc(nodes["w"], 16)
            sp.wait_ge(s_cols, 1)
            sp.dma_start(pen_d, pen[0:NG, :]).then_inc(nodes["cleared"], 16)
            sp.wait_ge(s_empty, 2)
            for k, tab in enumerate((tab0, tab1)):
                sp.dma_start(tab.rearrange("(p t) d -> p t d", p=P),
                             empty[:, k, :].unsqueeze(1).to_broadcast([P, NT, TABW])).then_inc(nodes["cleared"], 16)

        @block.gpsimd
        def _(pool):
            pool.memset(ident[:, :], 0.0).then_inc(s_id, 1)
            pool.wait_ge(s_id, 1)
            pool.affine_select(out=ident[:, :], in_=ident[:, :], compare_op=ALU.not_equal, fill=1.0,
                               base=0, pattern=[[-1, P]], channel_multiplier=1).then_inc(s_id, 1)
            pool.iota(keep["iotai"][:, :], pattern=[[1, ROWS]], base=0, channel_multiplier=0).then_inc(s_id, 1)

        @block.vector
        def _(v):
            v.memset(srci[:, :], 0).then_inc(s_clear, 1)
            v.memset(dsti[:, :], int(PAD_DST)).then_inc(s_clear, 1)
            v.memset(dirs[:, :, :], 0.0).then_inc(s_clear, 1)
            v.memset(nodes["x"][:, NT - 1, :], 0.0).then_inc(s_clear, 1)
            v.memset(empty[:, :, :], 0.0).then_inc(s_empty, 1)
            v.wait_ge(s_empty, 1)
            v.memset(empty[:, 1, 260:TABW], FAR).then_inc(s_empty, 1)
            v.memset(cut[:, 0:1], 0.0)
            v.memset(cut[:, ROWS:ROWS + 1], 0.0)
            v.wait_ge(s_id, 3)
            v.tensor_copy(keep["iota"][:, :], keep["iotai"][:, :])
            v.wait_ge(s_load, 96)
            v.tensor_copy(srcf[:, :], srci[:, :])
            v.tensor_copy(dstf[:, :], dsti[:, :]).then_inc(s_cut, 1)
            v.wait_ge(s_cut, 1)
            v.tensor_tensor(cut[:, 1:ROWS], dstf[:, 0:ROWS - 1], dstf[:, 1:ROWS], ALU.not_equal)
            v.tensor_scalar(dstc[:, :], dstf[:, :], float(N - 1), None, ALU.min).then_inc(s_cut, 1)
            v.wait_ge(s_cut, 2)
            v.tensor_scalar(pen[:, :], cut[:, :], FAR, None, ALU.mult)
            v.tensor_tensor_scan(rank[:, ::-1], cut[:, ROWS:0:-1], cut[:, ROWS:0:-1], 0.0, ALU.add, ALU.max)
            v.scalar_tensor_tensor(out=didx[:, :], in0=dstf[:, :], scalar=-PAD_DST, in1=cut[:, 1:ROWS + 1],
                                   op0=ALU.add, op1=ALU.mult).then_inc(s_cols, 1)
            v.wait_ge(s_cols, 1)
            v.tensor_scalar(nrank[:, :], rank[:, :], -1.0, None, ALU.mult).then_inc(s_cols, 1)
            for n, (_, _, out) in enumerate(jobs):
                v.wait_ge(s_tr, n + 1)
                v.tensor_copy(out, pt[n % 2][:, 0:4 * NG].rearrange("p (t g) -> p t g", t=4)).then_inc(s_ev, 1)
            v.wait_ge(s_tr, len(jobs) + 1)
            v.tensor_reduce(topf[:, 0:1], pt[0][0:1, 0:NG], AX.X, ALU.max).then_inc(s_top, 1)
            v.wait_ge(s_top, 1)
            v.tensor_copy(topi[:, :], topf[:, 0:1]).then_inc(s_top, 1)

        @block.tensor
        def _(pe):
            pe.wait_ge(s_id, 2)
            pe.wait_ge(s_cols, 2)
            for n, (a, half, _) in enumerate(jobs):
                at_least(pe, s_ev, n - 1)
                for t in range(4):
                    lo = (4 * half + t) * P
                    last = pe.transpose(pt[n % 2][:, t * NG:(t + 1) * NG], a[0:NG, lo:lo + P], ident[0:NG, 0:NG])
                last.then_inc(s_tr, 1)
            pe.wait_ge(s_ev, len(jobs))
            pe.transpose(pt[0][0:1, 0:NG], rank[0:NG, 0:1], ident[0:NG, 0:NG]).then_inc(s_tr, 1)


WAYS = 4


def live_tile(i):
    return not isinstance(i, int) or 0 <= i < NT


def norm_sums(v, i, b, x, st, mv, q):
    v.bn_stats(st[b][:, :], x).then_inc(q["stats"], 1)
    hold(v, q["stats"], i + 1, q["passed"])
    v.bn_aggr(mv[b][:, :], st[b][:, :]).then_inc(q["mv"], 1)


def norm_factors(v, i, b, mv, nrm, q):
    v.wait_ge(q["root"], i + 1)
    v.reciprocal(nrm[b][:, 0:1], nrm[b][:, 2:3]).then_inc(q["recip"], 1)
    v.wait_ge(q["recip"], i + 1)
    v.scalar_tensor_tensor(out=nrm[b][:, 1:2], in0=mv[b][:, 0:1], scalar=-1.0, in1=nrm[b][:, 0:1],
                           op0=ALU.mult, op1=ALU.mult).then_inc(q["nrm"], 1)


def norm_root(a, i, b, mv, nrm, eps, q):
    a.wait_ge(q["mv"], i + 1)
    a.activation(nrm[b][:, 2:3], mv[b][:, 1:2], ACT.Sqrt, bias=eps[:, 0:1]).then_inc(q["root"], 1)


def norm_relu(a, i, b, x, h, nrm, q):
    hold(a, q["nrm"], i + 1, q["relu"])
    hold(a, q["turned"], i + 1 - WAYS, q["relu"])
    a.activation(h[b][:, :], x, ACT.Relu, bias=nrm[b][:, 1:2], scale=nrm[b][:, 0:1]).then_inc(q["h"], 1)


def turn(pe, i, b, h, hps, ident, q):
    pe.wait_ge(q["h"], i + 1)
    at_least(pe, q["hT"], i - 1)
    for k in range(2):
        last = pe.transpose(hps[b % 2][:, k * P:(k + 1) * P], h[b][:, k * P:(k + 1) * P], ident[:, :])
    last.then_inc(q["turned"], 1)


def copy_turned(a, i, b, hps, hT, q):
    a.wait_ge(q["turned"], i + 1)
    at_least(a, q["proj"], i + 1 - WAYS)
    a.activation(hT[b][:, :], hps[b % 2][:, 0:D], ACT.Copy).then_inc(q["hT"], 1)


def project_nodes(nc, keep, nodes, q_d, kv_d, skip_d):
    with ExitStack() as ctx:
        m = Scope(nc, ctx)
        X, W, bias = nodes["x"], nodes["W"], nodes["bias"]
        ways = range(WAYS)
        h = [m.sb(f"h{b}", [P, D]) for b in ways]
        hT = [m.sb(f"hT{b}", [P, D]) for b in ways]
        res = [m.sb(f"res{b}", [P, 4 * D]) for b in ways]
        st = [m.sb(f"st{b}", [P, 6]) for b in ways]
        mv = [m.sb(f"mv{b}", [P, 2]) for b in ways]
        nrm = [m.sb(f"nrm{b}", [P, 3]) for b in ways]
        eps = m.sb("eps", [P, 1])
        hps = [m.ps(f"hps{b}", [P, 512]) for b in range(2)]
        proj = [m.ps(f"proj{b}", [P, 4 * D]) for b in range(2)]
        q = {n: m.sem(f"n0_{n}") for n in ("passed", "relu", "stats", "mv", "root", "recip", "nrm", "h", "turned", "hT",
                                           "proj", "sum", "res", "scaled", "eps")}
        s_out = [m.sem(f"n0_out{b}") for b in ways]
        ident = keep["ident"]
        block = ctx.enter_context(nc.Block())

        @block.sync
        def _(sp):
            def store(i, b):
                sp.wait_ge(q["res"], i + 1)
                rows = bass.ds(i * P, P)
                sp.dma_start(q_d[rows, :], res[b][:, 0:D]).then_inc(s_out[b], 16)
                sp.dma_start(kv_d[rows, :], res[b][:, D:3 * D]).then_inc(s_out[b], 16)
                sp.dma_start(skip_d[rows, :], res[b][:, 3 * D:]).then_inc(s_out[b], 16)

            sweep(sp, store, WAYS, NT - 1, NT, WAYS)
            for b in ways:
                sp.wait_ge(s_out[b], 48 * ((NT + WAYS - 1 - b) // WAYS))
            sp.wait_ge(nodes["cleared"], 48)

        @block.vector
        def _(v):
            v.memset(eps[:, :], 1e-5).then_inc(q["eps"], 1)

            def finish(i, b):
                v.wait_ge(q["proj"], i + 1)
                if not (isinstance(i, int) and i < WAYS):
                    v.wait_ge(s_out[b], uses(i, b, 48, WAYS) - 48)
                for k in range(2):
                    last = v.tensor_tensor(res[b][:, k * 512:(k + 1) * 512], proj[b % 2][:, k * 512:(k + 1) * 512],
                                           bias[:, k * 512:(k + 1) * 512], ALU.add)
                last.then_inc(q["sum"], 1)
                v.wait_ge(q["sum"], i + 1)
                v.tensor_tensor(res[b][:, 3 * D:], res[b][:, 3 * D:], X[:, i, :], ALU.add).then_inc(q["res"], 1)

            def step(i, b):
                if live_tile(i):
                    norm_sums(v, i, b, X[:, i, :], st, mv, q)
                if live_tile(i - 1):
                    norm_factors(v, i - 1, (b - 1) % WAYS, mv, nrm, q)
                if isinstance(i, int) and i == 1:
                    v.wait_ge(nodes["w"], 128)
                    v.tensor_scalar(W[:, :, 0:D], W[:, :, 0:D], 32.0 ** -0.5, None, ALU.mult)
                    v.tensor_scalar(bias[:, 0:D], bias[:, 0:D], 32.0 ** -0.5, None, ALU.mult).then_inc(q["scaled"], 1)
                    v.wait_ge(q["scaled"], 1)
                if live_tile(i - 3):
                    finish(i - 3, (b - 3) % WAYS)

            v.wait_ge(nodes["loaded"], 32)
            sweep(v, step, 2 * WAYS, NT - 1, NT + 3, WAYS)

        @block.scalar
        def _(a):
            a.wait_ge(q["eps"], 1)

            def step(i, b):
                if live_tile(i):
                    norm_root(a, i, b, mv, nrm, eps, q)
                if live_tile(i - 1):
                    norm_relu(a, i - 1, (b - 1) % WAYS, X[:, i - 1, :], h, nrm, q)
                if live_tile(i - 2):
                    copy_turned(a, i - 2, (b - 2) % WAYS, hps, hT, q)

            sweep(a, step, 2 * WAYS, NT - 1, NT + 2, WAYS)

        @block.tensor
        def _(pe):
            def project(i, b):
                pe.wait_ge(q["hT"], i + 1)
                at_least(pe, q["sum"], i - 1)
                for n in range(2):
                    for k in range(2):
                        last = pe.matmul(proj[b % 2][:, n * 512:(n + 1) * 512], hT[b][:, k * P:(k + 1) * P],
                                         W[:, k, n * 512:(n + 1) * 512], start=(k == 0), stop=(k == 1))
                last.then_inc(q["proj"], 1)

            def step(i, b):
                if live_tile(i):
                    turn(pe, i, b, h, hps, ident, q)
                if isinstance(i, int) and i == 1:
                    pe.wait_ge(q["scaled"], 1)
                if live_tile(i - 1):
                    project(i - 1, (b - 1) % WAYS)

            sweep(pe, step, 2 * WAYS, NT - 1, NT + 1, WAYS)


def edge_layer(nc, keep, layer, pen_d, tab, kv_d=None, q_d=None, edge_attr=None, We_d=None, fr_d=None):
    first = layer == 0
    H = 8 if first else 4
    C = D // 8 if first else 64
    PARTS = 4 if first else 2
    TP = G // PARTS
    FRW = 2 * (C + H)
    DEN = D
    with ExitStack() as ctx:
        m = Scope(nc, ctx)
        L = f"L{layer}_"
        two = range(2)
        if first:
            KV = [m.sb(f"{L}KV{b}", [P, G, 2 * D]) for b in two]
            Q = [m.sb(f"{L}Q{b}", [P, G, D]) for b in two]
            ea = [m.sb(f"{L}ea{b}", [P, G, D]) for b in two]
            eaT = [m.sb(f"{L}eaT{b}", [P, 4 * P]) for b in two]
            We = m.sb(f"{L}We", [P, 2, D])
            VAL = [m.sb(f"{L}VE{b}", [P, G, D]) for b in two]
            T = [m.ps(f"{L}T{b}", [P, 512]) for b in two]
            Ep = [m.ps(f"{L}E{b}", [P, 512]) for b in two]
        else:
            FR = [m.sb(f"{L}FR{b}", [P, G, FRW]) for b in two]
            VAL = [m.sb(f"{L}M{b}", [P, G, C + H]) for b in two]
        idx = [m.sb(f"{L}idx{b}", [P, G, 2], I32) for b in two]
        alpha = [m.sb(f"{L}alpha{b}", [P, G, H]) for b in two]
        pen = [m.sb(f"{L}pen{b}", [H, ROWS + 1]) for b in two]
        fwd = m.sb(f"{L}fwd", [H, ROWS])
        top = [m.sb(f"{L}top{b}", [H, ROWS]) for b in two]
        dif = [m.sb(f"{L}dif{b}", [P, (G + 1) * H]) for b in two]
        far = m.sb(f"{L}far", [H, 1])
        wgt = [m.sb(f"{L}wgt{b}", [P, (G + 1) * H]) for b in two]
        msg = [m.sb(f"{L}msg{b}", [P, G, MSGW]) for b in two]
        mask = [m.sb(f"{L}mask{b}", [P, G, P]) for b in two]
        O = [m.sb(f"{L}O{b}", [P, TABW]) for b in two]
        node = [m.sb(f"{L}node{b}", [P, 1], I32) for b in two]
        opened = [m.sb(f"{L}open{b}", [1, DEN + H]) for b in two]
        carry = [m.sb(f"{L}carry{b}", [1, DEN + H]) for b in two]
        turned = m.ps(f"{L}aT", [P, ROWS])
        back = m.ps(f"{L}back", [P, 512])
        Op = m.ps(f"{L}Op", [P, 512])

        names = ["passed", "ve", "prod", "alpha", "fwd", "top", "dif", "aT", "back", "before", "wgt", "row0", "den",
                 "msg", "dist", "mask", "carry", "sum", "rows", "idx", "setup"]
        names += ["we", "kj", "t", "tT", "e"] if first else []
        s = {n: m.sem(L + n) for n in names}
        s_in = [[m.sem(f"{L}in{b}_{p}") for p in range(PARTS)] for b in two]
        s_ea = [m.sem(f"{L}ea_in{b}") for b in two] if first else None
        s_pen = [m.sem(f"{L}pen_in{b}") for b in two]
        s_put = [m.sem(f"{L}put{b}") for b in two]
        per_part = 16 * TP * (2 if first else 1)
        ident, metaf, metai, iota = keep["ident"], keep["metaf"], keep["metai"], keep["iota"]
        need_rounds = keep["top"]
        block = ctx.enter_context(nc.Block())

        def choose(eng, program):
            most = eng.value_load(need_rounds[0:1, 0:1])
            with eng.If(most < P):
                program(1)
            with eng.Else():
                program(ALL_ROUNDS)

        def live(i):
            return not isinstance(i, int) or 0 <= i < NG

        @block.sync
        def _(sp):
            if first:
                sp.dma_start(We[:, :, :], We_d.rearrange("(k p) n -> p k n", p=P)).then_inc(s["we"], 16)

            def step(i, b):
                if first:
                    at_least(sp, s["t"], 4 * (i - 1))
                    if isinstance(i, int) and i == NG - 1:
                        full = LAST_ROWS // P
                        lo = i * STEP
                        sp.dma_start(ea[b][:, 0:full, :], edge_attr[lo:lo + full * P, :].rearrange("(t p) d -> p t d", p=P)
                                     ).then_inc(s_ea[b], 16)
                        sp.dma_start(ea[b][0:LAST_ROWS % P, full, :], edge_attr[lo + full * P:E, :]).then_inc(s_ea[b], 16)
                    else:
                        sp.dma_start(ea[b][:, :, :], edge_attr[bass.ds(i * STEP, ROWS), :].rearrange(
                            "(t p) d -> p t d", p=P)).then_inc(s_ea[b], 16)
                at_least(sp, s["top"], i - 1)
                sp.dma_start(pen[b][:, :], pen_d[bass.ds(i, 1), :].to_broadcast([H, ROWS + 1])).then_inc(s_pen[b], 16)

            sweep(sp, step, 4, NG - 2, NG)

        @block.gpsimd
        def _(pool):
            def program(rounds):
                lag = 4 if rounds == 1 else 2

                def gather(i, b, p):
                    t0 = p * TP
                    hold(pool, s["alpha"], PARTS * (i - 2) + p + 1, s["passed"])
                    pool.tensor_copy(idx[b][:, t0:t0 + TP, :], metai[:, i, t0:t0 + TP, :]).then_inc(s["idx"], 1)
                    hold(pool, s["idx"], PARTS * i + p + 1, s["passed"])
                    for t in range(t0, t0 + TP):
                        if first:
                            pool.indirect_dma_start(out=KV[b][:, t, :], out_offset=None, in_=kv_d,
                                                    in_offset=bass.IndirectOffsetOnAxis(ap=idx[b][:, t, 0:1], axis=0)
                                                    ).then_inc(s_in[b][p], 16)
                            pool.indirect_dma_start(out=Q[b][:, t, :], out_offset=None, in_=q_d,
                                                    in_offset=bass.IndirectOffsetOnAxis(ap=idx[b][:, t, 1:2], axis=0)
                                                    ).then_inc(s_in[b][p], 16)
                        else:
                            pool.indirect_dma_start(out=FR[b][:, t, :], out_offset=None, in_=fr_d,
                                                    in_offset=bass.IndirectOffsetOnAxis(ap=idx[b][:, t, 0:1], axis=0)
                                                    ).then_inc(s_in[b][p], 16)

                def put(g, b):
                    for r in range(rounds):
                        c = b if rounds == 1 else r % 2
                        hold(pool, s["rows"], rounds * g + r + 1, s["passed"])
                        pool.indirect_dma_start(out=tab, out_offset=bass.IndirectOffsetOnAxis(ap=node[c][:, 0:1], axis=0),
                                                in_=O[c][:, :], in_offset=None, bounds_check=N - 1, oob_is_err=False
                                                ).then_inc(s_put[c], 16)

                def step(i, b):
                    for p in range(PARTS):
                        if live(i):
                            gather(i, b, p)
                        if p == PARTS // 2 - 1 and live(i - lag):
                            put(i - lag, b)

                sweep(pool, step, 4, NG - 2, NG + lag)
                for c in range(2):
                    pool.wait_ge(s_put[c], 16 * rounds * NG // 2)

            choose(pool, program)

        @block.tensor
        def _(pe):
            if first:
                pe.wait_ge(s["we"], 16)

            def program(rounds):
                def attr_turn(i, b, p):
                    n = 4 * i + p
                    if p == 0:
                        pe.wait_ge(s_ea[b], uses(i, b, 16) + (16 if isinstance(i, int) and i == NG - 1 else 0))
                    at_least(pe, s["tT"], n - 1)
                    for u in range(2):
                        for k in range(2):
                            last = pe.transpose(T[p % 2][:, (2 * u + k) * P:(2 * u + k + 1) * P],
                                                ea[b][:, 2 * p + u, k * P:(k + 1) * P], ident[:, :])
                    last.then_inc(s["t"], 1)

                def attr_project(i, b, p):
                    n = 4 * i + p
                    pe.wait_ge(s["tT"], n + 1)
                    at_least(pe, s["ve"], n - 1)
                    for u in range(2):
                        for k in range(2):
                            last = pe.matmul(Ep[p % 2][:, u * D:(u + 1) * D], eaT[p % 2][:, (2 * u + k) * P:(2 * u + k + 1) * P],
                                             We[:, k, :], start=(k == 0), stop=(k == 1))
                    last.then_inc(s["e"], 1)

                def attrs(i, b, p):
                    if not first or not live(i):
                        return
                    if p < 3:
                        attr_turn(i, b, p + 1)
                    elif live(i + 1):
                        attr_turn(i + 1, 1 - b, 0)
                    attr_project(i, b, p)

                def scores_turn(g, b):
                    pe.wait_ge(s["alpha"], PARTS * (g + 1))
                    at_least(pe, s["fwd"], g)
                    for t in range(G):
                        last = pe.transpose(turned[0:H, t * P:(t + 1) * P], alpha[b][:, t, :], ident[:, :])
                    last.then_inc(s["aT"], 1)

                def scores_back(g, b):
                    hold(pe, s["dif"], g, s["passed"])
                    hold(pe, s["top"], g + 1, s["passed"])
                    for t in range(G):
                        pe.transpose(back[:, t * H:(t + 1) * H], top[b][:, t * P:(t + 1) * P], ident[0:H, 0:H])
                    before = far[:, :] if isinstance(g, int) and g == 0 else top[1 - b][:, STEP:ROWS]
                    pe.transpose(back[0:1, G * H:(G + 1) * H], before, ident[0:H, 0:H]).then_inc(s["back"], 1)

                def run_sums(g, b):
                    pe.wait_ge(s["msg"], g + 1)
                    pe.wait_ge(s["den"], g + 1)
                    for r in range(rounds):
                        c = b if rounds == 1 else r % 2
                        pe.wait_ge(s["mask"], rounds * g + r + 1)
                        at_least(pe, s["rows"], rounds * g + r)
                        for t in range(G):
                            last = pe.matmul(Op[:, 0:MSGW], mask[c][:, t, :], msg[b][:, t, :], start=(t == 0),
                                             stop=(t == G - 1))
                            if t == 0 and not (isinstance(g, int) and g == 0):
                                pe.wait_ge(s["carry"], g)
                                pe.matmul(Op[:, 0:DEN + H], mask[c][0:1, 0, :], carry[b][:, :], start=False, stop=False)
                        last.then_inc(s["sum"], 1)

                def step(i, b):
                    attrs(i, b, 0)
                    if live(i - 1):
                        scores_turn(i - 1, 1 - b)
                    attrs(i, b, 1)
                    if first and live(i - 2):
                        run_sums(i - 2, b)
                    attrs(i, b, 2)
                    if live(i - 1):
                        scores_back(i - 1, 1 - b)
                    if not first and live(i - 2):
                        run_sums(i - 2, b)
                    attrs(i, b, 3)

                if first:
                    attr_turn(0, 0, 0)
                sweep(pe, step, 4, NG - 2, NG + 2)

            choose(pe, program)

        @block.scalar
        def _(a):
            def program(rounds):
                def attr_copy(i, b, p):
                    n = 4 * i + p
                    a.wait_ge(s["t"], n + 1)
                    at_least(a, s["e"], n - 1)
                    a.activation(eaT[p % 2][:, :], T[p % 2][:, :], ACT.Copy).then_inc(s["tT"], 1)

                def weights(g, b):
                    a.wait_ge(s["dif"], g + 1)
                    at_least(a, s["msg"], g - 1)
                    at_least(a, s["carry"], g - 2)
                    a.activation(wgt[b][:, 0:G * H], dif[b][:, 0:G * H], ACT.Exp)
                    a.activation(wgt[b][0:1, G * H:], dif[b][0:1, G * H:], ACT.Exp).then_inc(s["wgt"], 1)

                def side_columns(g, b):
                    at_least(a, s["sum"], rounds * (g - 1))
                    a.activation(msg[b][:, :, TABW:MSGW], metaf[:, g, DIDX * G:(DIDX + 1) * G].unsqueeze(2), ACT.Copy)
                    a.wait_ge(s["wgt"], g + 1)
                    at_least(a, s["row0"], g)
                    a.activation(msg[b][:, :, DEN:DEN + H], wgt[b][:, 0:G * H].rearrange("p (t h) -> p t h", h=H),
                                 ACT.Copy).then_inc(s["den"], 1)

                def rows(g, b, r):
                    c = b if rounds == 1 else r % 2
                    a.wait_ge(s["sum"], rounds * g + r + 1)
                    if rounds == 1:
                        if not (isinstance(g, int) and g < 2):
                            a.wait_ge(s_put[c], uses(g, b, 16) - 16)
                    else:
                        at_least(a, s_put[c], 16 * (4 * g + r // 2))
                    if r == 0:
                        at_least(a, s["carry"], g - 1)
                        a.activation(opened[b][:, :], Op[0:1, 0:DEN + H], ACT.Copy)
                    a.activation(node[c][:, :], Op[:, TABW:MSGW], ACT.Copy, bias=PAD_DST)
                    a.activation(O[c][:, :], Op[:, 0:TABW], ACT.Copy).then_inc(s["rows"], 1)

                def masks(g, b):
                    for r in range(rounds):
                        c = b if rounds == 1 else r % 2
                        n = rounds * g + r
                        hold(a, s["sum"], n - 1, s["passed"])
                        for t in range(G):
                            last = a.activation(mask[c][:, t, :], iota[:, r * P:(r + 1) * P], ACT.Abs,
                                                bias=metaf[:, g, NRANK * G + t:NRANK * G + t + 1])
                        last.then_inc(s["dist"], 1)
                        a.wait_ge(s["dist"], n + 1)
                        a.activation(mask[c][:, :, :], mask[c][:, :, :], ACT.Relu, bias=1.0, scale=-1.0
                                     ).then_inc(s["mask"], 1)
                        if rounds > 1:
                            rows(g, b, r)

                def step0(i, b):
                    if live(i):
                        attr_copy(i, b, 1)
                    if live(i - 2):
                        side_columns(i - 2, b)
                    if live(i):
                        attr_copy(i, b, 2)
                    if live(i - 2):
                        if rounds > 1:
                            masks(i - 2, b)
                        else:
                            rows(i - 2, b, 0)
                    if live(i):
                        attr_copy(i, b, 3)
                    if live(i - 1):
                        weights(i - 1, 1 - b)
                    if live(i + 1):
                        attr_copy(i + 1, 1 - b, 0)
                    if live(i - 1) and rounds == 1:
                        masks(i - 1, 1 - b)

                def step1(i, b):
                    if live(i - 2):
                        side_columns(i - 2, b)
                    if live(i - 1):
                        weights(i - 1, 1 - b)
                        if rounds == 1:
                            masks(i - 1, 1 - b)
                    if live(i - 2):
                        if rounds > 1:
                            masks(i - 2, b)
                        else:
                            rows(i - 2, b, 0)

                if first:
                    attr_copy(0, 0, 0)
                sweep(a, step0 if first else step1, 4, NG - 2, NG + 2)

            if first:
                assert DEN + H == TABW
            choose(a, program)

        @block.vector
        def _(v):
            v.memset(far[:, :], FAR).then_inc(s["setup"], 1)
            v.wait_ge(s["setup"], 1)

            def program(rounds):
                def form0(i, b, p):
                    n, ts = 4 * i + p, slice(2 * p, 2 * p + 2)
                    e = Ep[p % 2][:, :].rearrange("p (t d) -> p t d", t=2)
                    v.wait_ge(s["e"], n + 1)
                    v.wait_ge(s_in[b][p], uses(i, b, per_part))
                    v.tensor_tensor(KV[b][:, ts, 0:D], KV[b][:, ts, 0:D], e, ALU.add).then_inc(s["kj"], 1)
                    at_least(v, s["msg"], i - 1)
                    v.tensor_tensor(VAL[b][:, ts, :], KV[b][:, ts, D:], e, ALU.add).then_inc(s["ve"], 1)
                    v.wait_ge(s["kj"], n + 1)
                    v.tensor_tensor(Q[b][:, ts, :], Q[b][:, ts, :], KV[b][:, ts, 0:D], ALU.mult).then_inc(s["prod"], 1)
                    v.wait_ge(s["prod"], n + 1)
                    at_least(v, s["aT"], i - 1)
                    at_least(v, s["dif"], i - 1)
                    v.tensor_reduce(alpha[b][:, ts, :], Q[b][:, ts, :].rearrange("p t (h c) -> p t h c", c=C),
                                    AX.X, ALU.add).then_inc(s["alpha"], 1)

                def form1(i, b, p):
                    n, ts, w = 2 * i + p, slice(p * TP, p * TP + TP), C + H
                    v.wait_ge(s_in[b][p], uses(i, b, per_part))
                    for k, d in enumerate((DIR0, DIR1)):
                        part = FR[b][:, ts, k * w:(k + 1) * w]
                        amount = metaf[:, i, d * G + p * TP:d * G + p * TP + TP].unsqueeze(2).to_broadcast([P, TP, w])
                        last = v.tensor_tensor(part, part, amount, ALU.mult)
                    last.then_inc(s["prod"], 1)
                    v.wait_ge(s["prod"], n + 1)
                    at_least(v, s["msg"], i - 1)
                    v.tensor_tensor(VAL[b][:, ts, :], FR[b][:, ts, 0:w], FR[b][:, ts, w:], ALU.add).then_inc(s["ve"], 1)
                    v.wait_ge(s["ve"], n + 1)
                    at_least(v, s["aT"], i - 1)
                    at_least(v, s["dif"], i - 1)
                    sc = VAL[b][:, ts, C:]
                    v.scalar_tensor_tensor(out=alpha[b][:, ts, :], in0=sc, scalar=0.2, in1=sc, op0=ALU.mult,
                                           op1=ALU.max).then_inc(s["alpha"], 1)

                def scans(g, b):
                    before = far[:, 0:1] if isinstance(g, int) and g == 0 else top[1 - b][:, STEP:ROWS]
                    v.wait_ge(s_pen[b], uses(g, b, 16))
                    v.wait_ge(s["aT"], g + 1)
                    at_least(v, s["top"], g)
                    v.tensor_tensor_scan(fwd[:, :], pen[b][:, 0:ROWS], turned[0:H, :], before, ALU.add, ALU.max
                                         ).then_inc(s["fwd"], 1)
                    v.wait_ge(s["fwd"], g + 1)
                    at_least(v, s["back"], g)
                    v.tensor_tensor_scan(top[b][:, ::-1], pen[b][:, ROWS:0:-1], fwd[:, ::-1], FAR, ALU.add, ALU.max
                                         ).then_inc(s["top"], 1)

                def differences(g, b):
                    v.wait_ge(s["back"], g + 1)
                    at_least(v, s["wgt"], g - 1)
                    v.tensor_copy(dif[b][0:1, G * H:], back[0:1, G * H:(G + 1) * H]).then_inc(s["before"], 1)
                    v.tensor_tensor(dif[b][:, 0:G * H], alpha[b][:, :, :].rearrange("p t h -> p (t h)"),
                                    back[:, 0:G * H], ALU.subtract)
                    if not first:
                        at_least(v, s["sum"], rounds * (g - 1))
                        v.tensor_tensor(msg[b][:, :, DEN + H:DEN + 2 * H], back[:, 0:G * H].rearrange(
                            "p (t h) -> p t h", h=H), metaf[:, g, END * G:(END + 1) * G].unsqueeze(2).to_broadcast(
                            [P, G, H]), ALU.mult)
                    v.wait_ge(s["before"], g + 1)
                    v.tensor_tensor(dif[b][0:1, G * H:], dif[b][0:1, G * H:], back[0:1, 0:H], ALU.subtract
                                    ).then_inc(s["dif"], 1)

                def carried(g, b):
                    if isinstance(g, int) and g == 0:
                        return
                    v.wait_ge(s["rows"], rounds * (g - 1) + 1)
                    v.wait_ge(s["wgt"], g + 1)
                    at_least(v, s["sum"], rounds * (g - 1))
                    f = wgt[b][0:1, G * H:(G + 1) * H]
                    v.tensor_tensor(carry[b][:, 0:DEN].rearrange("p (h c) -> p h c", c=C),
                                    opened[1 - b][:, 0:DEN].rearrange("p (h c) -> p h c", c=C),
                                    f.unsqueeze(2).to_broadcast([1, H, C]), ALU.mult)
                    v.tensor_tensor(carry[b][:, DEN:], opened[1 - b][:, DEN:], f, ALU.mult).then_inc(s["carry"], 1)

                def messages(g, b):
                    v.wait_ge(s["wgt"], g + 1)
                    if not (isinstance(g, int) and g == 0):
                        v.memset(wgt[b][0:1, 0:H], 0.0).then_inc(s["row0"], 1)
                        v.wait_ge(s["row0"], g)
                    at_least(v, s["sum"], rounds * (g - 1))
                    w4 = wgt[b][:, 0:G * H].rearrange("p (t h) -> p t h", h=H).unsqueeze(3).to_broadcast([P, G, H, C])
                    v.wait_ge(s["ve"], PARTS * (g + 1))
                    if first:
                        val = VAL[b][:, :, :].rearrange("p t (h c) -> p t h c", c=C)
                    else:
                        val = VAL[b][:, :, 0:C].unsqueeze(2).to_broadcast([P, G, H, C])
                    v.tensor_tensor(msg[b][:, :, 0:DEN].rearrange("p t (h c) -> p t h c", c=C), val, w4, ALU.mult
                                    ).then_inc(s["msg"], 1)

                form = form0 if first else form1

                def step(i, b):
                    order = [0, None, 1, "scans", 2, "dif", 3] if first else ["scans", None, 0, "dif", 1]
                    for what in order:
                        if what is None:
                            if live(i - 2):
                                carried(i - 2, b)
                        elif what == "scans":
                            if live(i - 1):
                                scans(i - 1, 1 - b)
                        elif what == "dif":
                            if live(i - 1):
                                differences(i - 1, 1 - b)
                        elif live(i):
                            form(i, b, what)
                    if live(i - 1):
                        messages(i - 1, 1 - b)

                sweep(v, step, 4, NG - 2, NG + 2)

            choose(v, program)


def between(nc, keep, x1, skip_d, tab0, Wf, Wr, attn, fr_d):
    H, C = 8, 32
    F, H1 = 64, 4
    FW = F + H1
    with ExitStack() as ctx:
        m = Scope(nc, ctx)
        ways = range(WAYS)
        wrows = m.sb("wrows", [F, 2, D])
        arow = m.sb("arow", [H1, F])
        acol = m.sb("acol", [F, H1])
        W = m.sb("Wfr", [P, 2, 2 * FW])
        inv = m.sb("b_inv", [P, NT, H])
        A = m.sb("b_A", [P, NT, TABW])
        h = [m.sb(f"b_h{b}", [P, D]) for b in ways]
        hT = [m.sb(f"b_hT{b}", [P, D]) for b in ways]
        fr = [m.sb(f"b_fr{b}", [P, 2 * FW]) for b in ways]
        st = [m.sb(f"b_st{b}", [P, 6]) for b in ways]
        mv = [m.sb(f"b_mv{b}", [P, 2]) for b in ways]
        nrm = [m.sb(f"b_nrm{b}", [P, 3]) for b in ways]
        eps = m.sb("b_eps", [P, 1])
        hps = [m.ps(f"b_hps{b}", [P, 512]) for b in range(2)]
        proj = [m.ps(f"b_proj{b}", [P, 512]) for b in range(2)]
        wps = m.ps("wps", [P, 512])
        q = {n: m.sem(f"n1_{n}") for n in ("passed", "stats", "mv", "root", "recip", "nrm", "h", "turned", "hT", "proj",
                                           "fr", "w", "eps", "inv", "scaled", "x1", "prep", "preped", "relu")}
        s_in = [m.sem(f"n1_in{b}") for b in range(2)]
        s_fr = [m.sem(f"n1_frout{b}") for b in ways]
        ident = keep["ident"]
        halves = (slice(0, 2 * WAYS), slice(2 * WAYS, NT))
        block = ctx.enter_context(nc.Block())

        @block.sync
        def _(sp):
            for half, ts in enumerate(halves):
                rows = slice(ts.start * P, ts.stop * P)
                sp.dma_start(A[:, ts, :], tab0[rows, :].rearrange("(t p) d -> p t d", p=P)).then_inc(s_in[half], 16)
                sp.dma_start(x1[:, ts, :], skip_d[rows, :].rearrange("(t p) d -> p t d", p=P)).then_inc(s_in[half], 16)
                if half == 0:
                    for n, w in enumerate((Wf, Wr)):
                        sp.dma_start(wrows[:, n, :], w).then_inc(q["w"], 16)
                    sp.dma_start(arow[:, :], attn.rearrange("a h f -> (a h) f")).then_inc(q["w"], 16)

            def store(i, b):
                hold(sp, q["fr"], i + 1, q["passed"])
                sp.dma_start(fr_d[bass.ds(i * P, P), :], fr[b][:, :]).then_inc(s_fr[b], 16)

            sweep(sp, store, WAYS, NT - 1, NT, WAYS)
            for b in ways:
                sp.wait_ge(s_fr[b], 16 * ((NT + WAYS - 1 - b) // WAYS))

        @block.gpsimd
        def _(pool):
            def scale(i):
                acc = A[:, i, 0:D].rearrange("p (h c) -> p h c", c=C)
                pool.tensor_tensor(acc, acc, inv[:, i, :].unsqueeze(2).to_broadcast([P, H, C]), ALU.mult
                                   ).then_inc(q["scaled"], 1)

            for half, ts in enumerate(halves):
                pool.wait_ge(q["inv"], 2 * half + 2)
                with pool.Fori(ts.start, ts.stop) as i:
                    scale(i)

        @block.vector
        def _(v):
            v.memset(eps[:, :], 1e-5).then_inc(q["eps"], 1)
            v.wait_ge(q["prep"], 1)
            v.tensor_copy(acol[:, :], wps[0:F, 0:H1]).then_inc(q["preped"], 1)
            v.wait_ge(q["prep"], 2)
            v.tensor_copy(W[:, :, :].rearrange("p k n -> p (k n)"), wps[:, 0:4 * FW]).then_inc(q["preped"], 1)
            for half, ts in enumerate(halves):
                v.wait_ge(s_in[half], 32)
                v.tensor_scalar(inv[:, ts, :], A[:, ts, D:D + H], 1e-16, None, ALU.add).then_inc(q["inv"], 1)
                v.wait_ge(q["inv"], 2 * half + 1)
                v.reciprocal(inv[:, ts, :], inv[:, ts, :]).then_inc(q["inv"], 1)

            def step(i, b):
                if live_tile(i):
                    v.wait_ge(q["scaled"], i + 1)
                    v.tensor_tensor(x1[:, i, :], x1[:, i, :], A[:, i, 0:D], ALU.add).then_inc(q["x1"], 1)
                    hold(v, q["x1"], i + 1, q["passed"])
                    norm_sums(v, i, b, x1[:, i, :], st, mv, q)
                if live_tile(i - 1):
                    norm_factors(v, i - 1, (b - 1) % WAYS, mv, nrm, q)

            sweep(v, step, 2 * WAYS, NT - 1, NT + 1, WAYS)

        @block.scalar
        def _(a):
            a.wait_ge(q["eps"], 1)

            def copy_rows(i, b):
                a.wait_ge(q["proj"], i + 1)
                if not (isinstance(i, int) and i < WAYS):
                    a.wait_ge(s_fr[b], uses(i, b, 16, WAYS) - 16)
                a.activation(fr[b][:, :], proj[b % 2][:, 0:2 * FW], ACT.Copy).then_inc(q["fr"], 1)

            def step(i, b):
                if live_tile(i):
                    norm_root(a, i, b, mv, nrm, eps, q)
                if live_tile(i - 1):
                    norm_relu(a, i - 1, (b - 1) % WAYS, x1[:, i - 1, :], h, nrm, q)
                if live_tile(i - 2):
                    copy_turned(a, i - 2, (b - 2) % WAYS, hps, hT, q)
                if live_tile(i - 3):
                    copy_rows(i - 3, (b - 3) % WAYS)

            sweep(a, step, 2 * WAYS, NT - 1, NT + 3, WAYS)

        @block.tensor
        def _(pe):
            pe.wait_ge(q["w"], 48)
            pe.transpose(wps[0:F, 0:H1], arow[:, :], ident[0:H1, 0:H1]).then_inc(q["prep"], 1)
            pe.wait_ge(q["preped"], 1)
            for k in range(2):
                for n in range(2):
                    at = (2 * k + n) * FW
                    half = wrows[:, n, k * P:(k + 1) * P]
                    pe.transpose(wps[:, at:at + F], half, ident[0:F, 0:F])
                    last = pe.matmul(wps[:, at + F:at + FW], half, acol[:, :], start=True, stop=True)
            last.then_inc(q["prep"], 1)
            pe.wait_ge(q["preped"], 2)

            def project(i, b):
                pe.wait_ge(q["hT"], i + 1)
                at_least(pe, q["fr"], i - 1)
                for k in range(2):
                    last = pe.matmul(proj[b % 2][:, 0:2 * FW], hT[b][:, k * P:(k + 1) * P], W[:, k, :],
                                     start=(k == 0), stop=(k == 1))
                last.then_inc(q["proj"], 1)

            def step(i, b):
                if live_tile(i):
                    turn(pe, i, b, h, hps, ident, q)
                if live_tile(i - 1):
                    project(i - 1, (b - 1) % WAYS)

            sweep(pe, step, 2 * WAYS, NT - 1, NT + 1, WAYS)


def finish(nc, keep, x1, tab1, out):
    H, C = 4, 64
    PER = 7
    chunks = [slice(t, min(t + PER, NT)) for t in range(0, NT, PER)]
    with ExitStack() as ctx:
        m = Scope(nc, ctx)
        A = m.sb("f_A", [P, NT, TABW])
        w = m.sb("f_w", [P, NT, H])
        f = m.sb("f_f", [P, NT, H])
        mcol = m.sb("f_mcol", [P, H])
        grow = m.sb("f_grow", [H, 1])
        diag = m.sb("f_diag", [H, H])
        ones = m.sb("f_ones", [H, P])
        gmax = m.sb("f_gmax", [P, H])
        ps = m.ps("f_ps", [P, 512])
        q = {n: m.sem(f"n2_{n}") for n in ("in", "col", "colT", "row", "diag", "g", "gm", "ones", "sub", "exp", "fac",
                                           "prod", "even", "odd", "out")}
        ident = keep["ident"]
        block = ctx.enter_context(nc.Block())

        def add(eng, c, done):
            eng.wait_ge(q["prod"], c + 1)
            eng.tensor_tensor(A[:, chunks[c], 0:D], A[:, chunks[c], 0:D], x1[:, chunks[c], :], ALU.add
                              ).then_inc(done, 1)

        @block.sync
        def _(sp):
            for ts in (slice(0, NT // 2), slice(NT // 2, NT)):
                sp.dma_start(A[:, ts, :], tab1[ts.start * P:ts.stop * P, :].rearrange("(t p) d -> p t d", p=P)
                             ).then_inc(q["in"], 16)
            stores = 0
            for c, ts in enumerate(chunks):
                sp.wait_ge(q["odd"] if c % 2 else q["even"], c // 2 + 1)
                full = min(ts.stop, NT - 1)
                sp.dma_start(out[ts.start * P:full * P, :].rearrange("(t p) d -> p t d", p=P),
                             A[:, ts.start:full, 0:D]).then_inc(q["out"], 16)
                stores += 1
                if ts.stop == NT:
                    sp.dma_start(out[full * P:N, :], A[0:LAST_NODES, full, 0:D]).then_inc(q["out"], 16)
                    stores += 1
            sp.wait_ge(q["out"], 16 * stores)

        @block.gpsimd
        def _(pool):
            for c in range(1, len(chunks), 2):
                add(pool, c, q["odd"])

        @block.tensor
        def _(pe):
            pe.wait_ge(q["col"], 1)
            pe.transpose(ps[0:H, 0:P], mcol[:, :], ident[:, :]).then_inc(q["colT"], 1)
            pe.wait_ge(q["diag"], 1)
            pe.matmul(ps[:, P:P + H], ones[:, :], diag[:, :], start=True, stop=True).then_inc(q["g"], 1)

        @block.scalar
        def _(a):
            a.wait_ge(q["sub"], 1)
            a.activation(w[:, :, :], w[:, :, :], ACT.Exp).then_inc(q["exp"], 1)

        @block.vector
        def _(v):
            DEN, MAX = A[:, :, D:D + H], A[:, :, D + H:TABW]
            v.memset(ones[:, :], 1.0).then_inc(q["ones"], 1)
            v.wait_ge(q["in"], 32)
            v.tensor_reduce(mcol[:, :], MAX.rearrange("p t h -> p h t"), AX.X, ALU.max).then_inc(q["col"], 1)
            v.wait_ge(q["colT"], 1)
            v.tensor_reduce(grow[:, :], ps[0:H, 0:P], AX.X, ALU.max).then_inc(q["row"], 1)
            v.wait_ge(q["row"], 1)
            v.tensor_scalar(diag[:, :], ident[0:H, 0:H], grow[:, 0:1], None, ALU.mult).then_inc(q["diag"], 1)
            v.wait_ge(q["g"], 1)
            v.tensor_copy(gmax[:, :], ps[:, P:P + H]).then_inc(q["gm"], 1)
            v.wait_ge(q["gm"], 1)
            v.tensor_tensor(w[:, :, :], MAX, gmax[:, :].unsqueeze(1).to_broadcast([P, NT, H]), ALU.subtract
                            ).then_inc(q["sub"], 1)
            v.wait_ge(q["exp"], 1)
            v.tensor_tensor(f[:, :, :], DEN, w[:, :, :], ALU.mult).then_inc(q["fac"], 1)
            v.wait_ge(q["fac"], 1)
            v.tensor_scalar(f[:, :, :], f[:, :, :], 1e-10, None, ALU.add).then_inc(q["fac"], 1)
            v.wait_ge(q["fac"], 2)
            v.reciprocal(f[:, :, :], f[:, :, :]).then_inc(q["fac"], 1)
            v.wait_ge(q["fac"], 3)
            v.tensor_tensor(f[:, :, :], f[:, :, :], w[:, :, :], ALU.mult).then_inc(q["fac"], 1)
            v.wait_ge(q["fac"], 4)
            for c, ts in enumerate(chunks):
                acc = A[:, ts, 0:D].rearrange("p t (h c) -> p t h c", c=C)
                v.tensor_tensor(acc, acc, f[:, ts, :].unsqueeze(3).to_broadcast([P, ts.stop - ts.start, H, C]), ALU.mult
                                ).then_inc(q["prod"], 1)
                if c % 2 == 0:
                    add(v, c, q["even"])


def build(nc, x, src, dst, edge_attr_2, edge_attr_256, Wq, bq, Wk, bk, Wv, bv, We, Ws, bs, Wf, Wr, attn, out):
    def scratch(name, shape):
        return nc.dram_tensor(name, shape, F32, kind="Internal").ap()

    q_d, kv_d, skip_d = scratch("q_d", [NPAD, D]), scratch("kv_d", [NPAD, 2 * D]), scratch("skip_d", [NPAD, D])
    fr_d = scratch("fr_d", [NPAD, 136])
    tab0, tab1 = scratch("tab0", [NPAD, TABW]), scratch("tab1", [NPAD, TABW])
    pen_d = scratch("pen_d", [NG, ROWS + 1])
    with ExitStack() as ctx:
        m = Scope(nc, ctx)
        keep = {
            "ident": m.sb("ident", [P, P]),
            "iotai": m.sb("iotai", [P, ROWS], I32),
            "iota": m.sb("iota", [P, ROWS]),
            "metaf": m.sb("metaf", [P, NG, NF * G]),
            "metai": m.sb("metai", [P, NG, G, 2], I32),
            "top": m.sb("most_runs", [1, 1], I32),
        }
        with ExitStack() as inner:
            n = Scope(nc, inner)
            nodes = {"x": n.sb("x_all", [P, NT, D]), "W": n.sb("Wqkvs", [P, 2, 4 * D]), "bias": n.sb("bias4", [P, 4 * D]),
                     "pen": n.sb("pen", [P, ROWS + 1]), "empty": n.sb("empty", [P, 2, TABW]),
                     "cleared": n.sem("tables_cleared"), "loaded": n.sem("x_loaded"), "w": n.sem("w_loaded")}
            prepare_edges(nc, keep, nodes, x, ((Wq, bq), (Wk, bk), (Wv, bv), (Ws, bs)), src, dst, edge_attr_2, pen_d,
                          tab0, tab1)
            project_nodes(nc, keep, nodes, q_d, kv_d, skip_d)
        edge_layer(nc, keep, 0, pen_d, tab0, kv_d=kv_d, q_d=q_d, edge_attr=edge_attr_256, We_d=We)
        x1 = m.sb("x1_all", [P, NT, D])
        between(nc, keep, x1, skip_d, tab0, Wf, Wr, attn, fr_d)
        edge_layer(nc, keep, 1, pen_d, tab1, fr_d=fr_d)
        finish(nc, keep, x1, tab1, out)


_INS = ["x", "src", "dst", "edge_attr_2", "edge_attr_256", "L0_gnn_Wq", "L0_gnn_bq", "L0_gnn_Wk", "L0_gnn_bk",
        "L0_gnn_Wv", "L0_gnn_bv", "L0_gnn_We", "L0_gnn_Ws", "L0_gnn_bs", "L1_gnn_W_forward", "L1_gnn_W_reverse",
        "L1_gnn_attn_forward"]


def kernel(**inputs):
    import numpy as _np
    import concourse.bacc as _bacc
    from concourse import mybir as _mybir
    from concourse.bass_utils import run_bass_kernel_spmd as _run

    nc = _bacc.Bacc("TRN2", target_bir_lowering=False, num_devices=1)
    arrays, args = {}, []
    for name in _INS:
        a = _np.ascontiguousarray(inputs[name])
        arrays[f"in_{name}_dram"] = a
        args.append(nc.dram_tensor(f"in_{name}_dram", a.shape, _mybir.dt.from_np(a.dtype), kind="ExternalInput").ap())
    args.append(nc.dram_tensor("out_0_dram", [N, D], F32, kind="ExternalOutput").ap())
    build(nc, *args)
    r = _run(nc, [arrays], core_ids=[0])
    return r.results[0]["out_0_dram"]
```

```python
from contextlib import ExitStack

import concourse.bass as bass
from concourse import mybir

P = 128
N, E, D = 6250, 106250, 256
NT = (N + P - 1) // P
NPAD = NT * P
LAST_NODES = N - (NT - 1) * P
G = 8
ROWS = G * P
STEP = ROWS - 1
NG = (E - 1 + STEP - 1) // STEP
LAST_ROWS = E - (NG - 1) * STEP
PAD_DST = 8191.0
FAR = -1e38
TABW = 264
MSGW = TABW + 1
ALL_ROUNDS = ROWS // P
XP = (1, 3)
XCOLS = len(XP) * 2 * P
assert NG <= P and LAST_ROWS < ROWS and NG % 4 == 0

NRANK, DIDX, END, DIR0, DIR1 = range(5)
NF = 5

ALU = mybir.AluOpType
ACT = mybir.ActivationFunctionType
AX = mybir.AxisListType
F32 = mybir.dt.float32
I32 = mybir.dt.int32


def at_least(eng, sem, value):
    if isinstance(value, int) and value <= 0:
        return
    eng.wait_ge(sem, value)


def hold(eng, sem, value, passed):
    at_least(eng, sem, value)
    if not isinstance(value, int):
        eng.sem_inc(passed, 1)


def sweep(eng, body, first, last, stop, ways=2):
    for i in range(first):
        body(i, i % ways)
    with eng.Fori(first // ways, last // ways) as turn_:
        for k in range(ways):
            body(turn_ * ways + k, k)
    for i in range(last, stop):
        body(i, i % ways)


def uses(g, buf, per_use, ways=2):
    return (g - buf) * (per_use // ways) + per_use


class Scope:

    def __init__(self, nc, ctx):
        self.nc, self.ctx = nc, ctx

    def sb(self, name, shape, dt=F32):
        return self.ctx.enter_context(self.nc.sbuf_tensor(name, shape, dt))

    def ps(self, name, shape):
        return self.ctx.enter_context(self.nc.psum_tensor(name, shape, F32))

    def sem(self, name):
        return self.ctx.enter_context(self.nc.semaphore(name))


def prepare_edges(nc, keep, nodes, x, weights, src, dst, edge_attr_2, pen_d, off_d, tab0, tab1):
    with ExitStack() as ctx:
        m = Scope(nc, ctx)
        srci, dsti = m.sb("srci", [P, ROWS], I32), m.sb("dsti", [P, ROWS], I32)
        srcf, dstf, dstc = m.sb("srcf", [P, ROWS]), m.sb("dstf", [P, ROWS]), m.sb("dstc", [P, ROWS])
        dirs = m.sb("dirs", [P, ROWS, 2])
        cut = m.sb("cut", [P, ROWS + 1])
        pen, empty = nodes["pen"], nodes["empty"]
        off = nodes["off"]
        low = m.sb("low", [P, 1])
        span = m.sb("span", [P, 1])
        pcoli = m.sb("pcoli", [P, 1], I32)
        rank, nrank, didx = m.sb("rank", [P, ROWS]), m.sb("nrank", [P, ROWS]), m.sb("didx", [P, ROWS])
        topf, topi = m.sb("topf", [1, 2]), keep["top"]
        pt = [m.ps(f"pt{b}", [P, 512]) for b in range(2)]
        s_clear, s_load, s_cols = m.sem("s_clear"), m.sem("s_load"), m.sem("s_cols")
        s_cut, s_id, s_tr, s_ev = m.sem("s_cut"), m.sem("s_id"), m.sem("s_tr"), m.sem("s_ev")
        s_top, s_empty, s_off = m.sem("s_top"), m.sem("s_empty"), m.sem("s_off")
        ident, metaf, ends = keep["ident"], keep["metaf"], keep["ends"]

        floats = {NRANK: nrank[:, :], DIDX: didx[:, :], END: cut[:, 1:ROWS + 1],
                  DIR0: dirs[:, :, 0], DIR1: dirs[:, :, 1]}
        jobs = []
        for half in range(2):
            for k, a in floats.items():
                out = metaf[:, :, k * G + 4 * half:k * G + 4 * half + 4].rearrange("p g t -> p t g")
                jobs.append((a, half, out))
            for k, a in ((0, srcf[:, :]), (1, dstc[:, :])):
                out = ends[:, :, 4 * half:4 * half + 4, k].rearrange("p g t -> p t g")
                jobs.append((a, half, out))
        block = ctx.enter_context(nc.Block())

        @block.sync
        def _(sp):
            sp.wait_ge(s_clear, 3)
            for flat, tile, w in ((src, srci[:, :], 1), (dst, dsti[:, :], 1),
                                  (edge_attr_2.rearrange("e c -> (e c)"), dirs[:, :, :].rearrange("p r c -> p (r c)"), 2)):
                rows = bass.AP(tensor=flat.tensor, offset=0, ap=[[STEP * w, NG - 1], [1, ROWS * w]])
                sp.dma_start(tile[0:NG - 1, :], rows).then_inc(s_load, 16)
                tail = flat[(NG - 1) * STEP * w:E * w].rearrange("(a b) -> a b", a=1)
                sp.dma_start(tile[NG - 1:NG, 0:LAST_ROWS * w], tail).then_inc(s_load, 16)
            sp.wait_ge(s_clear, 4)
            sp.dma_start(nodes["x"][:, 0:NT - 1, :], x[0:(NT - 1) * P, :].rearrange("(t p) d -> p t d", p=P)
                         ).then_inc(nodes["loaded"], 16)
            sp.dma_start(nodes["x"][0:LAST_NODES, NT - 1, :], x[(NT - 1) * P:N, :]).then_inc(nodes["loaded"], 16)
            for n, (w, b) in enumerate(weights):
                cols = slice(n * D, (n + 1) * D)
                sp.dma_start(nodes["W"][:, :, cols], w.rearrange("(k p) n -> p k n", p=P)).then_inc(nodes["w"], 16)
                sp.dma_start(nodes["bias"][:, cols], b.rearrange("(a n) -> a n", a=1).to_broadcast([P, D])
                             ).then_inc(nodes["w"], 16)
            sp.wait_ge(s_cols, 1)
            sp.dma_start(pen_d, pen[0:NG, :]).then_inc(nodes["cleared"], 16)
            sp.wait_ge(s_off, 3)
            for n, p in enumerate(XP):
                sp.dma_start(off_d[:, n * 2 * P:(n + 1) * 2 * P], off[0:NG, p * 2 * P:(p + 1) * 2 * P]
                             ).then_inc(nodes["cleared"], 16)
            sp.wait_ge(s_empty, 2)
            for k, tab in enumerate((tab0, tab1)):
                sp.dma_start(tab.rearrange("(p t) d -> p t d", p=P),
                             empty[:, k, :].unsqueeze(1).to_broadcast([P, NT, TABW])).then_inc(nodes["cleared"], 16)

        @block.gpsimd
        def _(pool):
            pool.memset(ident[:, :], 0.0).then_inc(s_id, 1)
            pool.wait_ge(s_id, 1)
            pool.affine_select(out=ident[:, :], in_=ident[:, :], compare_op=ALU.not_equal, fill=1.0,
                               base=0, pattern=[[-1, P]], channel_multiplier=1).then_inc(s_id, 1)
            pool.iota(keep["iotai"][:, :], pattern=[[1, ROWS]], base=0, channel_multiplier=0).then_inc(s_id, 1)
            pool.iota(pcoli[:, :], pattern=[[0, 1]], base=0, channel_multiplier=1).then_inc(s_id, 1)

        @block.vector
        def _(v):
            v.memset(srci[:, :], 0).then_inc(s_clear, 1)
            v.memset(dsti[:, :], int(PAD_DST)).then_inc(s_clear, 1)
            v.memset(dirs[:, :, :], 0.0).then_inc(s_clear, 1)
            v.memset(nodes["x"][:, NT - 1, :], 0.0).then_inc(s_clear, 1)
            v.memset(empty[:, :, :], 0.0).then_inc(s_empty, 1)
            v.wait_ge(s_empty, 1)
            v.memset(empty[:, 1, 260:TABW], FAR).then_inc(s_empty, 1)
            v.memset(cut[:, 0:1], 0.0)
            v.memset(cut[:, ROWS:ROWS + 1], 0.0)
            v.wait_ge(s_id, 4)
            v.tensor_copy(keep["iota"][:, :], keep["iotai"][:, :])
            v.tensor_copy(keep["pcol"][:, :], pcoli[:, :])
            v.wait_ge(s_load, 96)
            v.tensor_copy(srcf[:, :], srci[:, :])
            v.tensor_copy(dstf[:, :], dsti[:, :]).then_inc(s_cut, 1)
            v.wait_ge(s_cut, 1)
            v.tensor_tensor(cut[:, 1:ROWS], dstf[:, 0:ROWS - 1], dstf[:, 1:ROWS], ALU.not_equal)
            v.tensor_scalar(dstc[:, :], dstf[:, :], float(N - 1), None, ALU.min).then_inc(s_cut, 1)
            v.wait_ge(s_cut, 2)
            v.tensor_scalar(pen[:, :], cut[:, :], FAR, None, ALU.mult)
            v.tensor_tensor_scan(rank[:, ::-1], cut[:, ROWS:0:-1], cut[:, ROWS:0:-1], 0.0, ALU.add, ALU.max)
            v.scalar_tensor_tensor(out=didx[:, :], in0=dstf[:, :], scalar=-PAD_DST, in1=cut[:, 1:ROWS + 1],
                                   op0=ALU.add, op1=ALU.mult).then_inc(s_cols, 1)
            v.wait_ge(s_cols, 1)
            v.tensor_scalar(low[:, :], dstc[:, 0:1], float(NPAD - P), None, ALU.min).then_inc(s_off, 1)
            v.wait_ge(s_off, 1)
            v.tensor_scalar(off[:, :], dstc[:, :], low[:, 0:1], -1.0, ALU.subtract, ALU.mult).then_inc(s_off, 1)
            v.wait_ge(s_off, 2)
            v.scalar_tensor_tensor(out=span[:, :], in0=off[:, ROWS - 1:ROWS], scalar=-1.0, in1=rank[:, 0:1],
                                   op0=ALU.mult, op1=ALU.max).then_inc(s_off, 1)
            v.tensor_scalar(nrank[:, :], rank[:, :], -1.0, None, ALU.mult).then_inc(s_cols, 1)
            for n, (_, _, out) in enumerate(jobs):
                v.wait_ge(s_tr, n + 1)
                v.tensor_copy(out, pt[n % 2][:, 0:4 * NG].rearrange("p (t g) -> p t g", t=4)).then_inc(s_ev, 1)
            v.wait_ge(s_tr, len(jobs) + 1)
            v.tensor_reduce(topf[:, 0:1], pt[0][0:1, 0:NG], AX.X, ALU.max).then_inc(s_top, 1)
            v.wait_ge(s_top, 1)
            v.tensor_copy(topi[:, :], topf[:, 0:1]).then_inc(s_top, 1)
            v.tensor_copy(keep["low"][:, :], pt[0][0:1, P:P + NG]).then_inc(s_top, 1)

        @block.tensor
        def _(pe):
            pe.wait_ge(s_id, 2)
            pe.wait_ge(s_cols, 2)
            for n, (a, half, _) in enumerate(jobs):
                at_least(pe, s_ev, n - 1)
                for t in range(4):
                    lo = (4 * half + t) * P
                    last = pe.transpose(pt[n % 2][:, t * NG:(t + 1) * NG], a[0:NG, lo:lo + P], ident[0:NG, 0:NG])
                last.then_inc(s_tr, 1)
            pe.wait_ge(s_ev, len(jobs))
            pe.wait_ge(s_off, 3)
            pe.transpose(pt[0][0:1, P:P + NG], low[0:NG, :], ident[0:NG, 0:NG])
            pe.transpose(pt[0][0:1, 0:NG], span[0:NG, :], ident[0:NG, 0:NG]).then_inc(s_tr, 1)


WAYS = 4


def live_tile(i):
    return not isinstance(i, int) or 0 <= i < NT


def norm_sums(v, i, b, x, st, mv, q):
    v.bn_stats(st[b][:, :], x).then_inc(q["stats"], 1)
    hold(v, q["stats"], i + 1, q["passed"])
    v.bn_aggr(mv[b][:, :], st[b][:, :]).then_inc(q["mv"], 1)


def norm_factors(v, i, b, mv, nrm, q):
    v.wait_ge(q["root"], i + 1)
    v.reciprocal(nrm[b][:, 0:1], nrm[b][:, 2:3]).then_inc(q["recip"], 1)
    v.wait_ge(q["recip"], i + 1)
    v.scalar_tensor_tensor(out=nrm[b][:, 1:2], in0=mv[b][:, 0:1], scalar=-1.0, in1=nrm[b][:, 0:1],
                           op0=ALU.mult, op1=ALU.mult).then_inc(q["nrm"], 1)


def norm_root(a, i, b, mv, nrm, eps, q):
    a.wait_ge(q["mv"], i + 1)
    a.activation(nrm[b][:, 2:3], mv[b][:, 1:2], ACT.Sqrt, bias=eps[:, 0:1]).then_inc(q["root"], 1)


def norm_relu(a, i, b, x, h, nrm, q):
    hold(a, q["nrm"], i + 1, q["relu"])
    hold(a, q["turned"], i + 1 - WAYS, q["relu"])
    a.activation(h[b][:, :], x, ACT.Relu, bias=nrm[b][:, 1:2], scale=nrm[b][:, 0:1]).then_inc(q["h"], 1)


def turn(pe, i, b, h, hps, ident, q):
    pe.wait_ge(q["h"], i + 1)
    at_least(pe, q["hT"], i - 1)
    for k in range(2):
        last = pe.transpose(hps[b % 2][:, k * P:(k + 1) * P], h[b][:, k * P:(k + 1) * P], ident[:, :])
    last.then_inc(q["turned"], 1)


def copy_turned(a, i, b, hps, hT, q):
    a.wait_ge(q["turned"], i + 1)
    at_least(a, q["proj"], i + 1 - WAYS)
    a.activation(hT[b][:, :], hps[b % 2][:, 0:D], ACT.Copy).then_inc(q["hT"], 1)


def project_nodes(nc, keep, nodes, q_d, kv_d, skip_d):
    with ExitStack() as ctx:
        m = Scope(nc, ctx)
        X, W, bias = nodes["x"], nodes["W"], nodes["bias"]
        ways = range(WAYS)
        h = [m.sb(f"h{b}", [P, D]) for b in ways]
        hT = [m.sb(f"hT{b}", [P, D]) for b in ways]
        res = [m.sb(f"res{b}", [P, 4 * D]) for b in ways]
        st = [m.sb(f"st{b}", [P, 6]) for b in ways]
        mv = [m.sb(f"mv{b}", [P, 2]) for b in ways]
        nrm = [m.sb(f"nrm{b}", [P, 3]) for b in ways]
        eps = m.sb("eps", [P, 1])
        hps = [m.ps(f"hps{b}", [P, 512]) for b in range(2)]
        proj = [m.ps(f"proj{b}", [P, 4 * D]) for b in range(2)]
        q = {n: m.sem(f"n0_{n}") for n in ("passed", "relu", "stats", "mv", "root", "recip", "nrm", "h", "turned", "hT",
                                           "proj", "sum", "res", "scaled", "eps")}
        s_out = [m.sem(f"n0_out{b}") for b in ways]
        ident = keep["ident"]
        block = ctx.enter_context(nc.Block())

        @block.sync
        def _(sp):
            def store(i, b):
                sp.wait_ge(q["res"], i + 1)
                rows = bass.ds(i * P, P)
                sp.dma_start(q_d[rows, :], res[b][:, 0:D]).then_inc(s_out[b], 16)
                sp.dma_start(kv_d[rows, :], res[b][:, D:3 * D]).then_inc(s_out[b], 16)
                sp.dma_start(skip_d[rows, :], res[b][:, 3 * D:]).then_inc(s_out[b], 16)

            sweep(sp, store, WAYS, NT - 1, NT, WAYS)
            for b in ways:
                sp.wait_ge(s_out[b], 48 * ((NT + WAYS - 1 - b) // WAYS))
            sp.wait_ge(nodes["cleared"], 16 * (3 + len(XP)))

        @block.vector
        def _(v):
            v.memset(eps[:, :], 1e-5).then_inc(q["eps"], 1)

            def finish(i, b):
                v.wait_ge(q["proj"], i + 1)
                if not (isinstance(i, int) and i < WAYS):
                    v.wait_ge(s_out[b], uses(i, b, 48, WAYS) - 48)
                for k in range(2):
                    last = v.tensor_tensor(res[b][:, k * 512:(k + 1) * 512], proj[b % 2][:, k * 512:(k + 1) * 512],
                                           bias[:, k * 512:(k + 1) * 512], ALU.add)
                last.then_inc(q["sum"], 1)
                v.wait_ge(q["sum"], i + 1)
                v.tensor_tensor(res[b][:, 3 * D:], res[b][:, 3 * D:], X[:, i, :], ALU.add).then_inc(q["res"], 1)

            def step(i, b):
                if live_tile(i):
                    norm_sums(v, i, b, X[:, i, :], st, mv, q)
                if live_tile(i - 1):
                    norm_factors(v, i - 1, (b - 1) % WAYS, mv, nrm, q)
                if isinstance(i, int) and i == 1:
                    v.wait_ge(nodes["w"], 128)
                    v.tensor_scalar(W[:, :, 0:D], W[:, :, 0:D], 32.0 ** -0.5, None, ALU.mult)
                    v.tensor_scalar(bias[:, 0:D], bias[:, 0:D], 32.0 ** -0.5, None, ALU.mult).then_inc(q["scaled"], 1)
                    v.wait_ge(q["scaled"], 1)
                if live_tile(i - 3):
                    finish(i - 3, (b - 3) % WAYS)

            v.wait_ge(nodes["loaded"], 32)
            sweep(v, step, 2 * WAYS, NT - 1, NT + 3, WAYS)

        @block.scalar
        def _(a):
            a.wait_ge(q["eps"], 1)

            def step(i, b):
                if live_tile(i):
                    norm_root(a, i, b, mv, nrm, eps, q)
                if live_tile(i - 1):
                    norm_relu(a, i - 1, (b - 1) % WAYS, X[:, i - 1, :], h, nrm, q)
                if live_tile(i - 2):
                    copy_turned(a, i - 2, (b - 2) % WAYS, hps, hT, q)

            sweep(a, step, 2 * WAYS, NT - 1, NT + 2, WAYS)

        @block.tensor
        def _(pe):
            def project(i, b):
                pe.wait_ge(q["hT"], i + 1)
                at_least(pe, q["sum"], i - 1)
                for n in range(2):
                    for k in range(2):
                        last = pe.matmul(proj[b % 2][:, n * 512:(n + 1) * 512], hT[b][:, k * P:(k + 1) * P],
                                         W[:, k, n * 512:(n + 1) * 512], start=(k == 0), stop=(k == 1))
                last.then_inc(q["proj"], 1)

            def step(i, b):
                if live_tile(i):
                    turn(pe, i, b, h, hps, ident, q)
                if isinstance(i, int) and i == 1:
                    pe.wait_ge(q["scaled"], 1)
                if live_tile(i - 1):
                    project(i - 1, (b - 1) % WAYS)

            sweep(pe, step, 2 * WAYS, NT - 1, NT + 1, WAYS)


def edge_layer(nc, keep, layer, pen_d, tab, off_d=None, kv_d=None, q_d=None, edge_attr=None, We_d=None, fr_d=None):
    first = layer == 0
    H = 8 if first else 4
    C = D // 8 if first else 64
    PARTS = 4 if first else 2
    TP = G // PARTS
    FRW = 2 * (C + H)
    DEN = D
    with ExitStack() as ctx:
        m = Scope(nc, ctx)
        L = f"L{layer}_"
        two = range(2)
        if first:
            KV = [m.sb(f"{L}KV{b}", [P, G, 2 * D]) for b in two]
            Q = [m.sb(f"{L}Q{b}", [P, G, D]) for b in two]
            ea = [m.sb(f"{L}ea{b}", [P, G, D]) for b in two]
            eaT = [m.sb(f"{L}eaT{b}", [P, 4 * P]) for b in two]
            We = m.sb(f"{L}We", [P, 2, D])
            VAL = [m.sb(f"{L}VE{b}", [P, G, D]) for b in two]
            spread = [m.sb(f"{L}spread{b}", [P, XCOLS]) for b in two]
            Qn = [m.sb(f"{L}Qn{b}", [P, D]) for b in two]
            T = m.ps(f"{L}T", [P, 512])
            Qx = m.ps(f"{L}Qx", [P, 512])
            Ep = [m.ps(f"{L}E{b}", [P, 512]) for b in two]
        else:
            FR = [m.sb(f"{L}FR{b}", [P, G, FRW]) for b in two]
            VAL = [m.sb(f"{L}M{b}", [P, G, C + H]) for b in two]
        idx = [m.sb(f"{L}idx{b}", [P, G, 2], I32) for b in range(4)]
        alpha = [m.sb(f"{L}alpha{b}", [P, G, H]) for b in two]
        pen = [m.sb(f"{L}pen{b}", [H, ROWS + 1]) for b in two]
        fwd = m.sb(f"{L}fwd", [H, ROWS])
        top = [m.sb(f"{L}top{b}", [H, ROWS]) for b in two]
        dif = [m.sb(f"{L}dif{b}", [P, (G + 1) * H]) for b in two]
        far = m.sb(f"{L}far", [H, 1])
        wgt = [m.sb(f"{L}wgt{b}", [P, (G + 1) * H]) for b in two]
        msg = [m.sb(f"{L}msg{b}", [P, G, MSGW]) for b in two]
        mask = [m.sb(f"{L}mask{b}", [P, G, P]) for b in two]
        O = [m.sb(f"{L}O{b}", [P, TABW]) for b in two]
        node = [m.sb(f"{L}node{b}", [P, 1], I32) for b in two]
        opened = [m.sb(f"{L}open{b}", [1, DEN + H]) for b in two]
        turned = m.ps(f"{L}aT", [P, ROWS])
        back = m.ps(f"{L}back", [P, 512])
        Op = m.ps(f"{L}Op", [P, 512])

        names = ["passed", "ve", "prod", "alpha", "fwd", "top", "dif", "aT", "back", "before", "wgt", "den",
                 "msg", "dist", "mask", "carry", "sum", "rows", "idx", "setup"]
        names += ["we", "kj", "t", "tT", "e", "apart", "spread", "qx"] if first else []
        s = {n: m.sem(L + n) for n in names}
        s_in = [[m.sem(f"{L}in{b}_{p}") for p in range(PARTS)] for b in two]
        s_ea = [m.sem(f"{L}ea_in{b}") for b in two] if first else None
        s_q = [m.sem(f"{L}q_in{b}") for b in two] if first else None
        s_pen = [m.sem(f"{L}pen_in{b}") for b in two]
        s_put = [m.sem(f"{L}put{b}") for b in two]

        def gathers_q(p, rounds):
            return first and (rounds > 1 or p not in XP)

        ident, metaf, ends, iota = keep["ident"], keep["metaf"], keep["ends"], keep["iota"]
        need_rounds = keep["top"]
        block = ctx.enter_context(nc.Block())

        def choose(eng, program):
            most = eng.value_load(need_rounds[0:1, 0:1])
            with eng.If(most < P):
                program(1)
            with eng.Else():
                program(ALL_ROUNDS)

        def live(i):
            return not isinstance(i, int) or 0 <= i < NG

        @block.sync
        def _(sp):
            if first:
                sp.dma_start(We[:, :, :], We_d.rearrange("(k p) n -> p k n", p=P)).then_inc(s["we"], 16)

            def spread_in(i, b):
                low = sp.value_load(keep["low"][0:1, bass.ds(i, 1)], min_val=0, max_val=NPAD - P)
                at_least(sp, s["qx"], len(XP) * (i - 1))
                sp.dma_start(spread[b][:, :], off_d[bass.ds(i, 1), :].to_broadcast([P, XCOLS])).then_inc(s_q[b], 16)
                sp.dma_start(Qn[b][:, :], q_d[bass.ds(low, P), :]).then_inc(s_q[b], 16)

            def step(i, b, rounds):
                if first and rounds == 1:
                    spread_in(i, b)
                if first:
                    at_least(sp, s["t"], 4 * (i - 1))
                    if isinstance(i, int) and i == NG - 1:
                        full = LAST_ROWS // P
                        lo = i * STEP
                        sp.dma_start(ea[b][:, 0:full, :], edge_attr[lo:lo + full * P, :].rearrange("(t p) d -> p t d", p=P)
                                     ).then_inc(s_ea[b], 16)
                        sp.dma_start(ea[b][0:LAST_ROWS % P, full, :], edge_attr[lo + full * P:E, :]).then_inc(s_ea[b], 16)
                    else:
                        sp.dma_start(ea[b][:, :, :], edge_attr[bass.ds(i * STEP, ROWS), :].rearrange(
                            "(t p) d -> p t d", p=P)).then_inc(s_ea[b], 16)
                at_least(sp, s["top"], i - 1)
                sp.dma_start(pen[b][:, :], pen_d[bass.ds(i, 1), :].to_broadcast([H, ROWS + 1])).then_inc(s_pen[b], 16)

            choose(sp, lambda rounds: sweep(sp, lambda i, b: step(i, b, rounds), 4, NG - 2, NG))

        @block.gpsimd
        def _(pool):
            def program(rounds):
                lag = 4 if rounds == 1 else 2

                def gather(i, k, p):
                    b, t0 = k % 2, p * TP
                    if p == 0:
                        hold(pool, s["idx"], i + 1, s["passed"])
                    hold(pool, s["alpha"], PARTS * (i - 2) + p + 1, s["passed"])
                    for t in range(t0, t0 + TP):
                        if first:
                            pool.indirect_dma_start(out=KV[b][:, t, :], out_offset=None, in_=kv_d,
                                                    in_offset=bass.IndirectOffsetOnAxis(ap=idx[k][:, t, 0:1], axis=0)
                                                    ).then_inc(s_in[b][p], 16)
                        if gathers_q(p, rounds):
                            pool.indirect_dma_start(out=Q[b][:, t, :], out_offset=None, in_=q_d,
                                                    in_offset=bass.IndirectOffsetOnAxis(ap=idx[k][:, t, 1:2], axis=0)
                                                    ).then_inc(s_in[b][p], 16)
                        if not first:
                            pool.indirect_dma_start(out=FR[b][:, t, :], out_offset=None, in_=fr_d,
                                                    in_offset=bass.IndirectOffsetOnAxis(ap=idx[k][:, t, 0:1], axis=0)
                                                    ).then_inc(s_in[b][p], 16)

                def put(g, b):
                    for r in range(rounds):
                        c = b if rounds == 1 else r % 2
                        hold(pool, s["rows"], rounds * g + r + 1, s["passed"])
                        pool.indirect_dma_start(out=tab, out_offset=bass.IndirectOffsetOnAxis(ap=node[c][:, 0:1], axis=0),
                                                in_=O[c][:, :], in_offset=None, bounds_check=N - 1, oob_is_err=False
                                                ).then_inc(s_put[c], 16)

                def step(i, k):
                    for p in range(PARTS):
                        if live(i):
                            gather(i, k, p)
                        if p == PARTS // 2 - 1 and live(i - lag):
                            put(i - lag, k % 2)

                sweep(pool, step, 4, NG - 4, NG + lag, 4)
                for c in range(2):
                    pool.wait_ge(s_put[c], 16 * rounds * NG // 2)

            choose(pool, program)

        @block.tensor
        def _(pe):
            if first:
                pe.wait_ge(s["we"], 16)

            def program(rounds):
                def attr_turn(i, b, p):
                    n = 4 * i + p
                    if p == 0:
                        pe.wait_ge(s_ea[b], uses(i, b, 16) + (16 if isinstance(i, int) and i == NG - 1 else 0))
                    at_least(pe, s["tT"], n)
                    for u in range(2):
                        for k in range(2):
                            last = pe.transpose(T[:, (2 * u + k) * P:(2 * u + k + 1) * P],
                                                ea[b][:, 2 * p + u, k * P:(k + 1) * P], ident[:, :])
                    last.then_inc(s["t"], 1)

                def attr_project(i, b, p):
                    n = 4 * i + p
                    pe.wait_ge(s["tT"], n + 1)
                    at_least(pe, s["ve"], n - 1)
                    for u in range(2):
                        for k in range(2):
                            last = pe.matmul(Ep[p % 2][:, u * D:(u + 1) * D], eaT[p % 2][:, (2 * u + k) * P:(2 * u + k + 1) * P],
                                             We[:, k, :], start=(k == 0), stop=(k == 1))
                    last.then_inc(s["e"], 1)

                def attrs(i, b, p):
                    if not first or not live(i):
                        return
                    attr_project(i, b, p)
                    if p < 3:
                        attr_turn(i, b, p + 1)
                    elif live(i + 1):
                        attr_turn(i + 1, 1 - b, 0)

                def spread_q(i, b, p):
                    if not first or rounds > 1 or p not in XP or not live(i):
                        return
                    at_least(pe, s["spread"], i + 1)
                    k = XP.index(p)
                    at_least(pe, s["prod"], 4 * i + XP[k - 1] + 1 if k else 4 * (i - 1) + XP[-1] + 1)
                    for u in range(2):
                        lo = (2 * k + u) * P
                        last = pe.matmul(Qx[:, u * D:(u + 1) * D], spread[b][:, lo:lo + P], Qn[b][:, :], start=True, stop=True)
                    last.then_inc(s["qx"], 1)

                def scores_turn(g, b):
                    pe.wait_ge(s["alpha"], PARTS * (g + 1))
                    at_least(pe, s["fwd"], g)
                    for t in range(G):
                        last = pe.transpose(turned[0:H, t * P:(t + 1) * P], alpha[b][:, t, :], ident[:, :])
                    last.then_inc(s["aT"], 1)

                def scores_back(g, b):
                    hold(pe, s["dif"], g, s["passed"])
                    hold(pe, s["top"], g + 1, s["passed"])
                    for t in range(G):
                        pe.transpose(back[:, t * H:(t + 1) * H], top[b][:, t * P:(t + 1) * P], ident[0:H, 0:H])
                    before = far[:, :] if isinstance(g, int) and g == 0 else top[1 - b][:, STEP:ROWS]
                    pe.transpose(back[0:1, G * H:(G + 1) * H], before, ident[0:H, 0:H]).then_inc(s["back"], 1)

                def run_sums(g, b, half):
                    order = list(range(1, G)) + [0]
                    if rounds > 1:
                        tiles = order if half == (0 if first else 1) else []
                    else:
                        tiles = order[half * G // 2:(half + 1) * G // 2]
                    for r in range(rounds if tiles else 0):
                        c = b if rounds == 1 else r % 2
                        if order[0] in tiles:
                            if r == 0:
                                pe.wait_ge(s["msg"], g + 1)
                                pe.wait_ge(s["den"], g + 1)
                            pe.wait_ge(s["mask"], rounds * g + r + 1)
                            at_least(pe, s["rows"], rounds * g + r)
                        for t in tiles:
                            if t == 0:
                                at_least(pe, s["carry"], g)
                            last = pe.matmul(Op[:, 0:MSGW], mask[c][:, t, :], msg[b][:, t, :], start=(t == order[0]),
                                             stop=(t == order[-1]))
                        if order[-1] in tiles:
                            last.then_inc(s["sum"], 1)

                def step(i, b):
                    attrs(i, b, 0)
                    if live(i - 1):
                        scores_turn(i - 1, 1 - b)
                    attrs(i, b, 1)
                    spread_q(i, b, 1)
                    if live(i - 2):
                        run_sums(i - 2, b, 0)
                    attrs(i, b, 2)
                    spread_q(i, b, 3)
                    if live(i - 1):
                        scores_back(i - 1, 1 - b)
                    attrs(i, b, 3)
                    if live(i - 2):
                        run_sums(i - 2, b, 1)

                if first:
                    attr_turn(0, 0, 0)
                sweep(pe, step, 4, NG - 2, NG + 2)

            choose(pe, program)

        @block.scalar
        def _(a):
            def program(rounds):
                def attr_copy(i, b, p):
                    n = 4 * i + p
                    a.wait_ge(s["t"], n + 1)
                    at_least(a, s["e"], n - 1)
                    a.activation(eaT[p % 2][:, :], T[:, :], ACT.Copy).then_inc(s["tT"], 1)

                def indices(i, k):
                    if live(i):
                        a.activation(idx[k][:, :, :], ends[:, i, :, :], ACT.Copy).then_inc(s["idx"], 1)

                def weights(g, b):
                    a.wait_ge(s["dif"], g + 1)
                    at_least(a, s["msg"], g - 1)
                    at_least(a, s["carry"], g - 2)
                    a.activation(wgt[b][:, 0:G * H], dif[b][:, 0:G * H], ACT.Exp)
                    a.activation(wgt[b][0:1, G * H:], dif[b][0:1, G * H:], ACT.Exp).then_inc(s["wgt"], 1)

                def side_columns(g, b):
                    at_least(a, s["sum"], rounds * (g - 1))
                    a.activation(msg[b][:, :, TABW:MSGW], metaf[:, g, DIDX * G:(DIDX + 1) * G].unsqueeze(2), ACT.Copy)
                    a.wait_ge(s["wgt"], g + 1)
                    a.activation(msg[b][:, :, DEN:DEN + H], wgt[b][:, 0:G * H].rearrange("p (t h) -> p t h", h=H),
                                 ACT.Copy).then_inc(s["den"], 1)

                def rows(g, b, r):
                    c = b if rounds == 1 else r % 2
                    a.wait_ge(s["sum"], rounds * g + r + 1)
                    if rounds == 1:
                        if not (isinstance(g, int) and g < 2):
                            a.wait_ge(s_put[c], uses(g, b, 16) - 16)
                    else:
                        at_least(a, s_put[c], 16 * (4 * g + r // 2))
                    if r == 0:
                        at_least(a, s["carry"], g - 1)
                        a.activation(opened[b][:, :], Op[0:1, 0:DEN + H], ACT.Copy)
                    a.activation(node[c][:, :], Op[:, TABW:MSGW], ACT.Copy, bias=PAD_DST)
                    a.activation(O[c][:, :], Op[:, 0:TABW], ACT.Copy).then_inc(s["rows"], 1)

                def spread_masks(i, b):
                    if rounds > 1 or not live(i):
                        return
                    a.wait_ge(s_q[b], uses(i, b, 32))
                    a.activation(spread[b][:, :], spread[b][:, :], ACT.Abs, bias=keep["pcol"][:, 0:1]).then_inc(s["apart"], 1)
                    a.wait_ge(s["apart"], i + 1)
                    a.activation(spread[b][:, :], spread[b][:, :], ACT.Relu, bias=1.0, scale=-1.0).then_inc(s["spread"], 1)

                def masks(g, b, half=None):
                    for r in range(rounds):
                        c = b if rounds == 1 else r % 2
                        n = rounds * g + r
                        if half != 1:
                            hold(a, s["sum"], n - 1, s["passed"])
                        for t in range(G // 2 if half == 1 else 0, G // 2 if half == 0 else G):
                            last = a.activation(mask[c][:, t, :], iota[:, r * P:(r + 1) * P], ACT.Abs,
                                                bias=metaf[:, g, NRANK * G + t:NRANK * G + t + 1])
                        if half == 0:
                            return
                        last.then_inc(s["dist"], 1)
                        a.wait_ge(s["dist"], n + 1)
                        a.activation(mask[c][:, :, :], mask[c][:, :, :], ACT.Relu, bias=1.0, scale=-1.0
                                     ).then_inc(s["mask"], 1)
                        if rounds > 1:
                            rows(g, b, r)

                def step0(i, k):
                    b = k % 2
                    if live(i):
                        attr_copy(i, b, 1)
                    if live(i - 2) and rounds == 1:
                        masks(i - 2, b, 1)
                    if live(i - 2):
                        side_columns(i - 2, b)
                    if live(i):
                        attr_copy(i, b, 2)
                    if live(i - 2) and rounds > 1:
                        masks(i - 2, b)
                    if live(i):
                        attr_copy(i, b, 3)
                    if live(i - 1):
                        weights(i - 1, 1 - b)
                    indices(i + 2, (k + 2) % 4)
                    if live(i + 1):
                        attr_copy(i + 1, 1 - b, 0)
                    spread_masks(i + 1, 1 - b)
                    if live(i - 2) and rounds == 1:
                        rows(i - 2, b, 0)
                    if live(i - 1) and rounds == 1:
                        masks(i - 1, 1 - b, 0)

                def step1(i, k):
                    b = k % 2
                    if live(i - 2):
                        side_columns(i - 2, b)
                    if live(i - 1):
                        weights(i - 1, 1 - b)
                    indices(i + 2, (k + 2) % 4)
                    if live(i - 1) and rounds == 1:
                        masks(i - 1, 1 - b)
                    if live(i - 2):
                        if rounds > 1:
                            masks(i - 2, b)
                        else:
                            rows(i - 2, b, 0)

                indices(0, 0)
                indices(1, 1)
                if first:
                    attr_copy(0, 0, 0)
                    spread_masks(0, 0)
                sweep(a, step0 if first else step1, 4, NG - 4, NG + 2, 4)

            if first:
                assert DEN + H == TABW
            choose(a, program)

        @block.vector
        def _(v):
            v.memset(far[:, :], FAR).then_inc(s["setup"], 1)
            v.wait_ge(s["setup"], 1)

            def program(rounds):
                def form0(i, b, p):
                    n, ts = 4 * i + p, slice(2 * p, 2 * p + 2)
                    e = Ep[p % 2][:, :].rearrange("p (t d) -> p t d", t=2)
                    v.wait_ge(s["e"], n + 1)
                    v.wait_ge(s_in[b][p], uses(i, b, 16 * TP * (2 if gathers_q(p, rounds) else 1)))
                    v.tensor_tensor(KV[b][:, ts, 0:D], KV[b][:, ts, 0:D], e, ALU.add).then_inc(s["kj"], 1)
                    at_least(v, s["msg"], i - 1)
                    v.tensor_tensor(VAL[b][:, ts, :], KV[b][:, ts, D:], e, ALU.add).then_inc(s["ve"], 1)
                    v.wait_ge(s["kj"], n + 1)
                    if gathers_q(p, rounds):
                        qs = Q[b][:, ts, :]
                    else:
                        qs = Qx[:, :].rearrange("p (t d) -> p t d", t=2)
                        v.wait_ge(s["qx"], len(XP) * i + XP.index(p) + 1)
                    v.tensor_tensor(Q[b][:, ts, :], qs, KV[b][:, ts, 0:D], ALU.mult).then_inc(s["prod"], 1)
                    v.wait_ge(s["prod"], n + 1)
                    at_least(v, s["aT"], i - 1)
                    at_least(v, s["dif"], i - 1)
                    v.tensor_reduce(alpha[b][:, ts, :], Q[b][:, ts, :].rearrange("p t (h c) -> p t h c", c=C),
                                    AX.X, ALU.add).then_inc(s["alpha"], 1)

                def form1(i, b, p):
                    n, ts, w = 2 * i + p, slice(p * TP, p * TP + TP), C + H
                    v.wait_ge(s_in[b][p], uses(i, b, 16 * TP))
                    for k, d in enumerate((DIR0, DIR1)):
                        part = FR[b][:, ts, k * w:(k + 1) * w]
                        amount = metaf[:, i, d * G + p * TP:d * G + p * TP + TP].unsqueeze(2).to_broadcast([P, TP, w])
                        last = v.tensor_tensor(part, part, amount, ALU.mult)
                    last.then_inc(s["prod"], 1)
                    v.wait_ge(s["prod"], n + 1)
                    at_least(v, s["msg"], i - 1)
                    v.tensor_tensor(VAL[b][:, ts, :], FR[b][:, ts, 0:w], FR[b][:, ts, w:], ALU.add).then_inc(s["ve"], 1)
                    v.wait_ge(s["ve"], n + 1)
                    at_least(v, s["aT"], i - 1)
                    at_least(v, s["dif"], i - 1)
                    sc = VAL[b][:, ts, C:]
                    v.scalar_tensor_tensor(out=alpha[b][:, ts, :], in0=sc, scalar=0.2, in1=sc, op0=ALU.mult,
                                           op1=ALU.max).then_inc(s["alpha"], 1)

                def scans(g, b):
                    before = far[:, 0:1] if isinstance(g, int) and g == 0 else top[1 - b][:, STEP:ROWS]
                    v.wait_ge(s_pen[b], uses(g, b, 16))
                    v.wait_ge(s["aT"], g + 1)
                    at_least(v, s["top"], g)
                    v.tensor_tensor_scan(fwd[:, :], pen[b][:, 0:ROWS], turned[0:H, :], before, ALU.add, ALU.max
                                         ).then_inc(s["fwd"], 1)
                    v.wait_ge(s["fwd"], g + 1)
                    at_least(v, s["back"], g)
                    v.tensor_tensor_scan(top[b][:, ::-1], pen[b][:, ROWS:0:-1], fwd[:, ::-1], FAR, ALU.add, ALU.max
                                         ).then_inc(s["top"], 1)

                def differences(g, b):
                    v.wait_ge(s["back"], g + 1)
                    at_least(v, s["wgt"], g - 1)
                    v.tensor_copy(dif[b][0:1, G * H:], back[0:1, G * H:(G + 1) * H]).then_inc(s["before"], 1)
                    v.tensor_tensor(dif[b][:, 0:G * H], alpha[b][:, :, :].rearrange("p t h -> p (t h)"),
                                    back[:, 0:G * H], ALU.subtract)
                    if not first:
                        at_least(v, s["sum"], rounds * (g - 1))
                        v.tensor_tensor(msg[b][:, :, DEN + H:DEN + 2 * H], back[:, 0:G * H].rearrange(
                            "p (t h) -> p t h", h=H), metaf[:, g, END * G:(END + 1) * G].unsqueeze(2).to_broadcast(
                            [P, G, H]), ALU.mult)
                    v.wait_ge(s["before"], g + 1)
                    v.tensor_tensor(dif[b][0:1, G * H:], dif[b][0:1, G * H:], back[0:1, 0:H], ALU.subtract
                                    ).then_inc(s["dif"], 1)

                def carried(g, b):
                    if isinstance(g, int) and g == 0:
                        return
                    v.wait_ge(s["rows"], rounds * (g - 1) + 1)
                    v.wait_ge(s["msg"], g + 1)
                    v.wait_ge(s["den"], g + 1)
                    f = wgt[b][0:1, G * H:(G + 1) * H]
                    v.tensor_tensor(msg[b][0:1, 0, 0:DEN].rearrange("p (h c) -> p h c", c=C),
                                    opened[1 - b][:, 0:DEN].rearrange("p (h c) -> p h c", c=C),
                                    f.unsqueeze(2).to_broadcast([1, H, C]), ALU.mult)
                    v.tensor_tensor(msg[b][0:1, 0, DEN:DEN + H], opened[1 - b][:, DEN:], f, ALU.mult).then_inc(s["carry"], 1)

                def messages(g, b):
                    v.wait_ge(s["wgt"], g + 1)
                    at_least(v, s["sum"], rounds * (g - 1))
                    w4 = wgt[b][:, 0:G * H].rearrange("p (t h) -> p t h", h=H).unsqueeze(3).to_broadcast([P, G, H, C])
                    v.wait_ge(s["ve"], PARTS * (g + 1))
                    if first:
                        val = VAL[b][:, :, :].rearrange("p t (h c) -> p t h c", c=C)
                    else:
                        val = VAL[b][:, :, 0:C].unsqueeze(2).to_broadcast([P, G, H, C])
                    v.tensor_tensor(msg[b][:, :, 0:DEN].rearrange("p t (h c) -> p t h c", c=C), val, w4, ALU.mult
                                    ).then_inc(s["msg"], 1)

                form = form0 if first else form1

                def step(i, b):
                    order = [0, 1, "scans", None, 2, "dif", 3] if first else ["scans", None, 0, "dif", 1]
                    for what in order:
                        if what is None:
                            if live(i - 2):
                                carried(i - 2, b)
                        elif what == "scans":
                            if live(i - 1):
                                scans(i - 1, 1 - b)
                        elif what == "dif":
                            if live(i - 1):
                                differences(i - 1, 1 - b)
                        elif live(i):
                            form(i, b, what)
                    if live(i - 1):
                        messages(i - 1, 1 - b)

                sweep(v, step, 4, NG - 2, NG + 2)

            choose(v, program)


def between(nc, keep, x1, skip_d, tab0, Wf, Wr, attn, fr_d):
    H, C = 8, 32
    F, H1 = 64, 4
    FW = F + H1
    with ExitStack() as ctx:
        m = Scope(nc, ctx)
        ways = range(WAYS)
        wrows = m.sb("wrows", [F, 2, D])
        arow = m.sb("arow", [H1, F])
        acol = m.sb("acol", [F, H1])
        W = m.sb("Wfr", [P, 2, 2 * FW])
        inv = m.sb("b_inv", [P, NT, H])
        A = m.sb("b_A", [P, NT, TABW])
        h = [m.sb(f"b_h{b}", [P, D]) for b in ways]
        hT = [m.sb(f"b_hT{b}", [P, D]) for b in ways]
        fr = [m.sb(f"b_fr{b}", [P, 2 * FW]) for b in ways]
        st = [m.sb(f"b_st{b}", [P, 6]) for b in ways]
        mv = [m.sb(f"b_mv{b}", [P, 2]) for b in ways]
        nrm = [m.sb(f"b_nrm{b}", [P, 3]) for b in ways]
        eps = m.sb("b_eps", [P, 1])
        hps = [m.ps(f"b_hps{b}", [P, 512]) for b in range(2)]
        proj = [m.ps(f"b_proj{b}", [P, 512]) for b in range(2)]
        wps = m.ps("wps", [P, 512])
        q = {n: m.sem(f"n1_{n}") for n in ("passed", "stats", "mv", "root", "recip", "nrm", "h", "turned", "hT", "proj",
                                           "fr", "w", "eps", "inv", "scaled", "x1", "prep", "preped", "relu")}
        s_in = [m.sem(f"n1_in{b}") for b in range(2)]
        s_fr = [m.sem(f"n1_frout{b}") for b in ways]
        ident = keep["ident"]
        halves = (slice(0, 2 * WAYS), slice(2 * WAYS, NT))
        block = ctx.enter_context(nc.Block())

        @block.sync
        def _(sp):
            for half, ts in enumerate(halves):
                rows = slice(ts.start * P, ts.stop * P)
                sp.dma_start(A[:, ts, :], tab0[rows, :].rearrange("(t p) d -> p t d", p=P)).then_inc(s_in[half], 16)
                sp.dma_start(x1[:, ts, :], skip_d[rows, :].rearrange("(t p) d -> p t d", p=P)).then_inc(s_in[half], 16)
                if half == 0:
                    for n, w in enumerate((Wf, Wr)):
                        sp.dma_start(wrows[:, n, :], w).then_inc(q["w"], 16)
                    sp.dma_start(arow[:, :], attn.rearrange("a h f -> (a h) f")).then_inc(q["w"], 16)

            def store(i, b):
                hold(sp, q["fr"], i + 1, q["passed"])
                sp.dma_start(fr_d[bass.ds(i * P, P), :], fr[b][:, :]).then_inc(s_fr[b], 16)

            sweep(sp, store, WAYS, NT - 1, NT, WAYS)
            for b in ways:
                sp.wait_ge(s_fr[b], 16 * ((NT + WAYS - 1 - b) // WAYS))

        @block.gpsimd
        def _(pool):
            def scale(i):
                acc = A[:, i, 0:D].rearrange("p (h c) -> p h c", c=C)
                pool.tensor_tensor(acc, acc, inv[:, i, :].unsqueeze(2).to_broadcast([P, H, C]), ALU.mult
                                   ).then_inc(q["scaled"], 1)

            for half, ts in enumerate(halves):
                pool.wait_ge(q["inv"], 2 * half + 2)
                with pool.Fori(ts.start, ts.stop) as i:
                    scale(i)

        @block.vector
        def _(v):
            v.memset(eps[:, :], 1e-5).then_inc(q["eps"], 1)
            v.wait_ge(q["prep"], 1)
            v.tensor_copy(acol[:, :], wps[0:F, 0:H1]).then_inc(q["preped"], 1)
            v.wait_ge(q["prep"], 2)
            v.tensor_copy(W[:, :, :].rearrange("p k n -> p (k n)"), wps[:, 0:4 * FW]).then_inc(q["preped"], 1)
            for half, ts in enumerate(halves):
                v.wait_ge(s_in[half], 32)
                v.tensor_scalar(inv[:, ts, :], A[:, ts, D:D + H], 1e-16, None, ALU.add).then_inc(q["inv"], 1)
                v.wait_ge(q["inv"], 2 * half + 1)
                v.reciprocal(inv[:, ts, :], inv[:, ts, :]).then_inc(q["inv"], 1)

            def step(i, b):
                if live_tile(i):
                    v.wait_ge(q["scaled"], i + 1)
                    v.tensor_tensor(x1[:, i, :], x1[:, i, :], A[:, i, 0:D], ALU.add).then_inc(q["x1"], 1)
                    hold(v, q["x1"], i + 1, q["passed"])
                    norm_sums(v, i, b, x1[:, i, :], st, mv, q)
                if live_tile(i - 1):
                    norm_factors(v, i - 1, (b - 1) % WAYS, mv, nrm, q)

            sweep(v, step, 2 * WAYS, NT - 1, NT + 1, WAYS)

        @block.scalar
        def _(a):
            a.wait_ge(q["eps"], 1)

            def copy_rows(i, b):
                a.wait_ge(q["proj"], i + 1)
                if not (isinstance(i, int) and i < WAYS):
                    a.wait_ge(s_fr[b], uses(i, b, 16, WAYS) - 16)
                a.activation(fr[b][:, :], proj[b % 2][:, 0:2 * FW], ACT.Copy).then_inc(q["fr"], 1)

            def step(i, b):
                if live_tile(i):
                    norm_root(a, i, b, mv, nrm, eps, q)
                if live_tile(i - 1):
                    norm_relu(a, i - 1, (b - 1) % WAYS, x1[:, i - 1, :], h, nrm, q)
                if live_tile(i - 2):
                    copy_turned(a, i - 2, (b - 2) % WAYS, hps, hT, q)
                if live_tile(i - 3):
                    copy_rows(i - 3, (b - 3) % WAYS)

            sweep(a, step, 2 * WAYS, NT - 1, NT + 3, WAYS)

        @block.tensor
        def _(pe):
            pe.wait_ge(q["w"], 48)
            pe.transpose(wps[0:F, 0:H1], arow[:, :], ident[0:H1, 0:H1]).then_inc(q["prep"], 1)
            pe.wait_ge(q["preped"], 1)
            for k in range(2):
                for n in range(2):
                    at = (2 * k + n) * FW
                    half = wrows[:, n, k * P:(k + 1) * P]
                    pe.transpose(wps[:, at:at + F], half, ident[0:F, 0:F])
                    last = pe.matmul(wps[:, at + F:at + FW], half, acol[:, :], start=True, stop=True)
            last.then_inc(q["prep"], 1)
            pe.wait_ge(q["preped"], 2)

            def project(i, b):
                pe.wait_ge(q["hT"], i + 1)
                at_least(pe, q["fr"], i - 1)
                for k in range(2):
                    last = pe.matmul(proj[b % 2][:, 0:2 * FW], hT[b][:, k * P:(k + 1) * P], W[:, k, :],
                                     start=(k == 0), stop=(k == 1))
                last.then_inc(q["proj"], 1)

            def step(i, b):
                if live_tile(i):
                    turn(pe, i, b, h, hps, ident, q)
                if live_tile(i - 1):
                    project(i - 1, (b - 1) % WAYS)

            sweep(pe, step, 2 * WAYS, NT - 1, NT + 1, WAYS)


def finish(nc, keep, x1, tab1, out):
    H, C = 4, 64
    PER = 7
    chunks = [slice(t, min(t + PER, NT)) for t in range(0, NT, PER)]
    with ExitStack() as ctx:
        m = Scope(nc, ctx)
        A = m.sb("f_A", [P, NT, TABW])
        w = m.sb("f_w", [P, NT, H])
        f = m.sb("f_f", [P, NT, H])
        mcol = m.sb("f_mcol", [P, H])
        grow = m.sb("f_grow", [H, 1])
        diag = m.sb("f_diag", [H, H])
        ones = m.sb("f_ones", [H, P])
        gmax = m.sb("f_gmax", [P, H])
        ps = m.ps("f_ps", [P, 512])
        q = {n: m.sem(f"n2_{n}") for n in ("in", "col", "colT", "row", "diag", "g", "gm", "ones", "sub", "exp", "fac",
                                           "prod", "even", "odd", "out")}
        ident = keep["ident"]
        block = ctx.enter_context(nc.Block())

        def add(eng, c, done):
            eng.wait_ge(q["prod"], c + 1)
            eng.tensor_tensor(A[:, chunks[c], 0:D], A[:, chunks[c], 0:D], x1[:, chunks[c], :], ALU.add
                              ).then_inc(done, 1)

        @block.sync
        def _(sp):
            for ts in (slice(0, NT // 2), slice(NT // 2, NT)):
                sp.dma_start(A[:, ts, :], tab1[ts.start * P:ts.stop * P, :].rearrange("(t p) d -> p t d", p=P)
                             ).then_inc(q["in"], 16)
            stores = 0
            for c, ts in enumerate(chunks):
                sp.wait_ge(q["odd"] if c % 2 else q["even"], c // 2 + 1)
                full = min(ts.stop, NT - 1)
                sp.dma_start(out[ts.start * P:full * P, :].rearrange("(t p) d -> p t d", p=P),
                             A[:, ts.start:full, 0:D]).then_inc(q["out"], 16)
                stores += 1
                if ts.stop == NT:
                    sp.dma_start(out[full * P:N, :], A[0:LAST_NODES, full, 0:D]).then_inc(q["out"], 16)
                    stores += 1
            sp.wait_ge(q["out"], 16 * stores)

        @block.gpsimd
        def _(pool):
            for c in range(1, len(chunks), 2):
                add(pool, c, q["odd"])

        @block.tensor
        def _(pe):
            pe.wait_ge(q["col"], 1)
            pe.transpose(ps[0:H, 0:P], mcol[:, :], ident[:, :]).then_inc(q["colT"], 1)
            pe.wait_ge(q["diag"], 1)
            pe.matmul(ps[:, P:P + H], ones[:, :], diag[:, :], start=True, stop=True).then_inc(q["g"], 1)

        @block.scalar
        def _(a):
            a.wait_ge(q["sub"], 1)
            a.activation(w[:, :, :], w[:, :, :], ACT.Exp).then_inc(q["exp"], 1)

        @block.vector
        def _(v):
            DEN, MAX = A[:, :, D:D + H], A[:, :, D + H:TABW]
            v.memset(ones[:, :], 1.0).then_inc(q["ones"], 1)
            v.wait_ge(q["in"], 32)
            v.tensor_reduce(mcol[:, :], MAX.rearrange("p t h -> p h t"), AX.X, ALU.max).then_inc(q["col"], 1)
            v.wait_ge(q["colT"], 1)
            v.tensor_reduce(grow[:, :], ps[0:H, 0:P], AX.X, ALU.max).then_inc(q["row"], 1)
            v.wait_ge(q["row"], 1)
            v.tensor_scalar(diag[:, :], ident[0:H, 0:H], grow[:, 0:1], None, ALU.mult).then_inc(q["diag"], 1)
            v.wait_ge(q["g"], 1)
            v.tensor_copy(gmax[:, :], ps[:, P:P + H]).then_inc(q["gm"], 1)
            v.wait_ge(q["gm"], 1)
            v.tensor_tensor(w[:, :, :], MAX, gmax[:, :].unsqueeze(1).to_broadcast([P, NT, H]), ALU.subtract
                            ).then_inc(q["sub"], 1)
            v.wait_ge(q["exp"], 1)
            v.tensor_tensor(f[:, :, :], DEN, w[:, :, :], ALU.mult).then_inc(q["fac"], 1)
            v.wait_ge(q["fac"], 1)
            v.tensor_scalar(f[:, :, :], f[:, :, :], 1e-10, None, ALU.add).then_inc(q["fac"], 1)
            v.wait_ge(q["fac"], 2)
            v.reciprocal(f[:, :, :], f[:, :, :]).then_inc(q["fac"], 1)
            v.wait_ge(q["fac"], 3)
            v.tensor_tensor(f[:, :, :], f[:, :, :], w[:, :, :], ALU.mult).then_inc(q["fac"], 1)
            v.wait_ge(q["fac"], 4)
            for c, ts in enumerate(chunks):
                acc = A[:, ts, 0:D].rearrange("p t (h c) -> p t h c", c=C)
                v.tensor_tensor(acc, acc, f[:, ts, :].unsqueeze(3).to_broadcast([P, ts.stop - ts.start, H, C]), ALU.mult
                                ).then_inc(q["prod"], 1)
                if c % 2 == 0:
                    add(v, c, q["even"])


def build(nc, x, src, dst, edge_attr_2, edge_attr_256, Wq, bq, Wk, bk, Wv, bv, We, Ws, bs, Wf, Wr, attn, out):
    def scratch(name, shape):
        return nc.dram_tensor(name, shape, F32, kind="Internal").ap()

    q_d, kv_d, skip_d = scratch("q_d", [NPAD, D]), scratch("kv_d", [NPAD, 2 * D]), scratch("skip_d", [NPAD, D])
    fr_d = scratch("fr_d", [NPAD, 136])
    tab0, tab1 = scratch("tab0", [NPAD, TABW]), scratch("tab1", [NPAD, TABW])
    pen_d, off_d = scratch("pen_d", [NG, ROWS + 1]), scratch("off_d", [NG, XCOLS])
    with ExitStack() as ctx:
        m = Scope(nc, ctx)
        keep = {
            "ident": m.sb("ident", [P, P]),
            "iotai": m.sb("iotai", [P, ROWS], I32),
            "iota": m.sb("iota", [P, ROWS]),
            "metaf": m.sb("metaf", [P, NG, NF * G]),
            "ends": m.sb("ends", [P, NG, G, 2]),
            "top": m.sb("most_runs", [1, 1], I32),
            "low": m.sb("low_rows", [1, NG], I32),
            "pcol": m.sb("pcol", [P, 1]),
        }
        with ExitStack() as inner:
            n = Scope(nc, inner)
            nodes = {"x": n.sb("x_all", [P, NT, D]), "W": n.sb("Wqkvs", [P, 2, 4 * D]), "bias": n.sb("bias4", [P, 4 * D]),
                     "pen": n.sb("pen", [P, ROWS + 1]), "empty": n.sb("empty", [P, 2, TABW]),
                     "off": n.sb("off", [P, ROWS]),
                     "cleared": n.sem("tables_cleared"), "loaded": n.sem("x_loaded"), "w": n.sem("w_loaded")}
            prepare_edges(nc, keep, nodes, x, ((Wq, bq), (Wk, bk), (Wv, bv), (Ws, bs)), src, dst, edge_attr_2, pen_d,
                          off_d, tab0, tab1)
            project_nodes(nc, keep, nodes, q_d, kv_d, skip_d)
        edge_layer(nc, keep, 0, pen_d, tab0, off_d=off_d, kv_d=kv_d, q_d=q_d, edge_attr=edge_attr_256, We_d=We)
        x1 = m.sb("x1_all", [P, NT, D])
        between(nc, keep, x1, skip_d, tab0, Wf, Wr, attn, fr_d)
        edge_layer(nc, keep, 1, pen_d, tab1, fr_d=fr_d)
        finish(nc, keep, x1, tab1, out)


_INS = ["x", "src", "dst", "edge_attr_2", "edge_attr_256", "L0_gnn_Wq", "L0_gnn_bq", "L0_gnn_Wk", "L0_gnn_bk",
        "L0_gnn_Wv", "L0_gnn_bv", "L0_gnn_We", "L0_gnn_Ws", "L0_gnn_bs", "L1_gnn_W_forward", "L1_gnn_W_reverse",
        "L1_gnn_attn_forward"]


def kernel(**inputs):
    import numpy as _np
    import concourse.bacc as _bacc
    from concourse import mybir as _mybir
    from concourse.bass_utils import run_bass_kernel_spmd as _run

    nc = _bacc.Bacc("TRN2", target_bir_lowering=False, num_devices=1)
    arrays, args = {}, []
    for name in _INS:
        a = _np.ascontiguousarray(inputs[name])
        arrays[f"in_{name}_dram"] = a
        args.append(nc.dram_tensor(f"in_{name}_dram", a.shape, _mybir.dt.from_np(a.dtype), kind="ExternalInput").ap())
    args.append(nc.dram_tensor("out_0_dram", [N, D], F32, kind="ExternalOutput").ap())
    build(nc, *args)
    r = _run(nc, [arrays], core_ids=[0])
    return r.results[0]["out_0_dram"]
```
